# Optimizing a Trainium2 kernel written in Bass

```python
import numpy as np
import jax
import jax.numpy as jnp

def _softmax(x, axis=-1):
    return jax.nn.softmax(x, axis=axis)

def _gelu(x):
    return jax.nn.gelu(x, approximate=True)

def _silu(x):
    return jax.nn.silu(x)

def _sigmoid(x):
    return jax.nn.sigmoid(x)

def _layernorm(x, axis=-1, eps=1e-05):
    m = jnp.mean(x, axis=axis, keepdims=True)
    v = jnp.var(x, axis=axis, keepdims=True)
    return (x - m) / jnp.sqrt(v + eps)

def _scatter_add(tgt, idx, src, axis=0):
    return tgt.at[idx].add(src)

def _segment_sum(src, seg, n):
    return jax.ops.segment_sum(src, seg, n)
kernel_name = 'mk_gnn_preln_d1_gnn_r32_c66ab1'

def setup_inputs(seed: int=0):
    np.random.seed(seed)
    _w = jnp.asarray

    def _rec_inputs():
        import jax
        import jax.numpy as jnp
        _gk = jax.random.key(seed)
        x = -0.000202 + 1 * jax.random.normal(jax.random.fold_in(_gk, 1), (3125, 128), jnp.float32)
        _s = jax.random.randint(jax.random.fold_in(_gk, 2), (25000,), 0, 3125, jnp.int32)
        _d = jax.random.randint(jax.random.fold_in(_gk, 3), (25000,), 0, 3125, jnp.int32)
        _loop = jnp.arange(3125, dtype=jnp.int32)
        src = jnp.concatenate([_s, _d, _loop])
        dst = jnp.concatenate([_d, _s, _loop])
        _o = jnp.argsort(dst, stable=True)
        src = src[_o]
        dst = dst[_o]
        edge_attr_10 = jax.random.uniform(jax.random.fold_in(_gk, 12), (53125, 10), jnp.float32, 0.0, 1)
        edge_attr_4 = 0.00109026 + 0.999989 * jax.random.normal(jax.random.fold_in(_gk, 13), (53125, 4), jnp.float32)
        node_vec1 = jax.random.uniform(jax.random.fold_in(_gk, 14), (3125, 1), jnp.float32, 0.0, 1)
        return (x, src, dst, edge_attr_10, edge_attr_4, node_vec1)
    x, src, dst, edge_attr_10, edge_attr_4, node_vec1 = _rec_inputs()

    def _L0_gnn_setup():
        import math
        import jax
        import jax.numpy as jnp
        import numpy as np
        MUL = 32
        N_NODES = 50000
        N_EDGES = 25000
        N_BASIS = 10
        N_HID = 100
        NUM_NEIGHBORS = 16.0

        def _fctp(x0, x1, attr, W0, W1):
            inv = 1.0 / math.sqrt(W0.shape[0])
            o0 = attr * (x0 @ W0) * inv
            o1 = attr[:, :, None] * jnp.einsum('nud,uw->nwd', x1, W1) * inv
            return (o0, o1)

        def _forward(node_input, node_attr, edge_attr, edge_length_embedded, W_sc0, W_sc1, W_l10, W_l11, W_l20, W_l21, W_fc1, W_fc2, edge_src, edge_dst):
            N = node_input.shape[0]
            x0 = node_input[:, :MUL]
            x1 = node_input[:, MUL:].reshape(N, MUL, 3)
            s0, s1 = _fctp(x0, x1, node_attr, W_sc0, W_sc1)
            y0, y1 = _fctp(x0, x1, node_attr, W_l10, W_l11)
            h = jax.nn.silu(edge_length_embedded @ W_fc1 * (1.0 / math.sqrt(N_BASIS)))
            w = h @ W_fc2 * (1.0 / math.sqrt(N_HID))
            w1, w2, w3, w4 = (w[:, 0 * MUL:1 * MUL], w[:, 1 * MUL:2 * MUL], w[:, 2 * MUL:3 * MUL], w[:, 3 * MUL:4 * MUL])
            x0s = y0[edge_src]
            x1s = y1[edge_src]
            ea0 = edge_attr[:, :1]
            ea1 = edge_attr[:, 1:]
            mid0a = w1 * x0s * ea0
            mid0b = w4 * jnp.einsum('eum,em->eu', x1s, ea1) * (1.0 / math.sqrt(3.0))
            mid1a = (w2 * x0s)[:, :, None] * ea1[:, None, :]
            mid1b = w3[:, :, None] * x1s * ea0[:, None, :]
            E = edge_attr.shape[0]
            edge_features = jnp.concatenate([mid0a, mid0b, mid1a.reshape(E, -1), mid1b.reshape(E, -1)], axis=1)
            agg = jax.ops.segment_sum(edge_features, edge_dst, num_segments=N)
            agg = agg * (1.0 / math.sqrt(NUM_NEIGHBORS))
            m0 = agg[:, :2 * MUL]
            m1 = agg[:, 2 * MUL:].reshape(N, 2 * MUL, 3)
            z0, z1 = _fctp(m0, m1, node_attr, W_l20, W_l21)
            c_s = math.sin(math.pi / 8.0)
            c_x = math.cos(math.pi / 8.0)
            out0 = c_s * s0 + c_x * z0
            out1 = c_s * s1 + c_x * z1
            return jnp.concatenate([out0, out1.reshape(N, -1)], axis=1)
        key = jax.random.key(seed)
        ks = jax.random.split(key, 14)
        return {'node_input': jax.random.normal(ks[0], (N_NODES, 4 * MUL), jnp.float32), 'node_attr': jnp.ones((N_NODES, 1), jnp.float32), 'edge_src': jax.random.randint(ks[1], (N_EDGES,), 0, N_NODES, dtype=jnp.int32), 'edge_dst': jax.random.randint(ks[2], (N_EDGES,), 0, N_NODES, dtype=jnp.int32), 'edge_attr': jax.random.normal(ks[3], (N_EDGES, 4), jnp.float32), 'edge_length_embedded': jax.random.uniform(ks[4], (N_EDGES, N_BASIS), dtype=jnp.float32), 'W_sc0': jax.random.normal(ks[5], (MUL, MUL), jnp.float32), 'W_sc1': jax.random.normal(ks[6], (MUL, MUL), jnp.float32), 'W_l10': jax.random.normal(ks[7], (MUL, MUL), jnp.float32), 'W_l11': jax.random.normal(ks[8], (MUL, MUL), jnp.float32), 'W_l20': jax.random.normal(ks[9], (2 * MUL, MUL), jnp.float32), 'W_l21': jax.random.normal(ks[10], (2 * MUL, MUL), jnp.float32), 'W_fc1': jax.random.normal(ks[11], (N_BASIS, N_HID), jnp.float32), 'W_fc2': jax.random.normal(ks[12], (N_HID, 4 * MUL), jnp.float32)}
    _L0_gnn_all = _L0_gnn_setup()
    _L0_gnn_in = {k: v for k, v in _L0_gnn_all.items() if k in ('W_sc0', 'W_sc1', 'W_l10', 'W_l11', 'W_l20', 'W_l21', 'W_fc1', 'W_fc2')}
    del _L0_gnn_all
    return {'x': x, 'src': src, 'dst': dst, 'edge_attr_10': edge_attr_10, 'edge_attr_4': edge_attr_4, 'node_vec1': node_vec1, 'L0_gnn_W_sc0': _L0_gnn_in['W_sc0'], 'L0_gnn_W_sc1': _L0_gnn_in['W_sc1'], 'L0_gnn_W_l10': _L0_gnn_in['W_l10'], 'L0_gnn_W_l11': _L0_gnn_in['W_l11'], 'L0_gnn_W_l20': _L0_gnn_in['W_l20'], 'L0_gnn_W_l21': _L0_gnn_in['W_l21'], 'L0_gnn_W_fc1': _L0_gnn_in['W_fc1'], 'L0_gnn_W_fc2': _L0_gnn_in['W_fc2']}

def reference(x, src, dst, edge_attr_10, edge_attr_4, node_vec1, L0_gnn_W_sc0, L0_gnn_W_sc1, L0_gnn_W_l10, L0_gnn_W_l11, L0_gnn_W_l20, L0_gnn_W_l21, L0_gnn_W_fc1, L0_gnn_W_fc2):
    import jax
    import jax.numpy as jnp

    def _L0_gnn_ref(node_input, node_attr, edge_src, edge_dst, edge_attr, edge_length_embedded, W_sc0, W_sc1, W_l10, W_l11, W_l20, W_l21, W_fc1, W_fc2):
        import math
        import jax
        import jax.numpy as jnp
        import numpy as np
        MUL = 32
        N_NODES = 50000
        N_EDGES = 25000
        N_BASIS = 10
        N_HID = 100
        NUM_NEIGHBORS = 16.0

        def _fctp(x0, x1, attr, W0, W1):
            inv = 1.0 / math.sqrt(W0.shape[0])
            o0 = attr * (x0 @ W0) * inv
            o1 = attr[:, :, None] * jnp.einsum('nud,uw->nwd', x1, W1) * inv
            return (o0, o1)

        def _forward(node_input, node_attr, edge_attr, edge_length_embedded, W_sc0, W_sc1, W_l10, W_l11, W_l20, W_l21, W_fc1, W_fc2, edge_src, edge_dst):
            N = node_input.shape[0]
            x0 = node_input[:, :MUL]
            x1 = node_input[:, MUL:].reshape(N, MUL, 3)
            s0, s1 = _fctp(x0, x1, node_attr, W_sc0, W_sc1)
            y0, y1 = _fctp(x0, x1, node_attr, W_l10, W_l11)
            h = jax.nn.silu(edge_length_embedded @ W_fc1 * (1.0 / math.sqrt(N_BASIS)))
            w = h @ W_fc2 * (1.0 / math.sqrt(N_HID))
            w1, w2, w3, w4 = (w[:, 0 * MUL:1 * MUL], w[:, 1 * MUL:2 * MUL], w[:, 2 * MUL:3 * MUL], w[:, 3 * MUL:4 * MUL])
            x0s = y0[edge_src]
            x1s = y1[edge_src]
            ea0 = edge_attr[:, :1]
            ea1 = edge_attr[:, 1:]
            mid0a = w1 * x0s * ea0
            mid0b = w4 * jnp.einsum('eum,em->eu', x1s, ea1) * (1.0 / math.sqrt(3.0))
            mid1a = (w2 * x0s)[:, :, None] * ea1[:, None, :]
            mid1b = w3[:, :, None] * x1s * ea0[:, None, :]
            E = edge_attr.shape[0]
            edge_features = jnp.concatenate([mid0a, mid0b, mid1a.reshape(E, -1), mid1b.reshape(E, -1)], axis=1)
            agg = jax.ops.segment_sum(edge_features, edge_dst, num_segments=N)
            agg = agg * (1.0 / math.sqrt(NUM_NEIGHBORS))
            m0 = agg[:, :2 * MUL]
            m1 = agg[:, 2 * MUL:].reshape(N, 2 * MUL, 3)
            z0, z1 = _fctp(m0, m1, node_attr, W_l20, W_l21)
            c_s = math.sin(math.pi / 8.0)
            c_x = math.cos(math.pi / 8.0)
            out0 = c_s * s0 + c_x * z0
            out1 = c_s * s1 + c_x * z1
            return jnp.concatenate([out0, out1.reshape(N, -1)], axis=1)
        return _forward(node_input, node_attr, edge_attr, edge_length_embedded, W_sc0, W_sc1, W_l10, W_l11, W_l20, W_l21, W_fc1, W_fc2, edge_src, edge_dst)
    h = jnp.maximum(_layernorm(x, axis=-1), 0.0)
    x = x + _L0_gnn_ref(h, node_vec1, src, dst, edge_attr_4, edge_attr_10, L0_gnn_W_sc0, L0_gnn_W_sc1, L0_gnn_W_l10, L0_gnn_W_l11, L0_gnn_W_l20, L0_gnn_W_l21, L0_gnn_W_fc1, L0_gnn_W_fc2)
    return x

_drawn_inputs = setup_inputs


def setup_inputs(seed=0):
    import zlib

    import numpy as np

    out = dict(_drawn_inputs(seed))
    spreads = {}
    factors = {}
    for name, (base, spread) in spreads.items():
        noise = np.random.default_rng([zlib.crc32(name.encode()), seed]).standard_normal(out[name].shape)
        drawn = base * np.exp(spread * noise) if base else spread * noise
        out[name] = jnp.asarray(drawn.astype(out[name].dtype))
    for name, factor in factors.items():
        out[name] = (out[name] * factor).astype(out[name].dtype)
    return out
```

```python
import math
from contextlib import ExitStack

import concourse.bass as bass
from concourse import mybir

P = 128
NODES, FEAT, MUL = 3125, 128, 32
EDGES, BASIS, HID = 53125, 10, 100
CHUNKS = -(-NODES // P)
NP = CHUNKS * P
TQ = 4
QE = TQ * P
QUADS = -(-EDGES // QE)
BODY = 8
SLOTS = 4
TURNS = QUADS // BODY
TILES = QUADS * TQ
WIN = 48
NK = 4
AHEAD = 2
LN_EPS = 1e-5
ROUND_UP = 0.51

assert QUADS % BODY == 0 and BODY % SLOTS == 0 and SLOTS % 2 == 0

C_SELF = math.sin(math.pi / 8) / math.sqrt(MUL)
C_AGG = (math.cos(math.pi / 8) / math.sqrt(2 * MUL) / math.sqrt(16.0)
         / math.sqrt(HID) / math.sqrt(MUL))
C_DOT = C_AGG / math.sqrt(3.0)
C_FC1 = 1.0 / math.sqrt(BASIS)

BATCHES = [(0, 4), (4, 8), (12, 8), (20, 5)]
GROUPS = [(c, min(4, CHUNKS - c)) for c in range(0, CHUNKS, 4)]

W_IN, W_SELF, W_AGG, W_DOT = 0, 128, 256, 384
W_COLS = W_DOT + 3 * 64
C_IDENT, C_IOTA = 0, 128
C_COLS = C_IOTA + WIN


def edge_conv_program(nc, x, attr, node_w, consts, fc1_w, fc2_w, src_idx, dst_tiles, dst_quads,
                      edge_at, lengths, y_table, out):
    f32, i32 = mybir.dt.float32, mybir.dt.int32
    ALU = mybir.AluOpType
    ACT = mybir.ActivationFunctionType
    AX = mybir.AxisListType

    ctx = ExitStack()
    with ctx:
        def sb(name, shape, dt=f32):
            return ctx.enter_context(nc.sbuf_tensor(name, shape, dt))

        def pb(name):
            return ctx.enter_context(nc.psum_tensor(name, [P, 512], f32))

        def sem(name):
            return ctx.enter_context(nc.semaphore(name))

        x_sb = sb("x_sb", [P, CHUNKS, FEAT])
        attr_sb = sb("attr_sb", [P, CHUNKS])
        stats = sb("stats", [P, CHUNKS, 6])
        m_sum = sb("m_sum", [P, CHUNKS])
        m_diff = sb("m_diff", [P, CHUNKS])
        v_sum = sb("v_sum", [P, CHUNKS])
        m_sq = sb("m_sq", [P, CHUNKS])
        mean = sb("mean", [P, CHUNKS])
        var = sb("var", [P, CHUNKS])
        std = sb("std", [P, CHUNKS])
        rstd = sb("rstd", [P, CHUNKS])
        xn = sb("xn", [P, CHUNKS, FEAT])
        h_t = sb("h_t", [P, CHUNKS, P])
        y_sb = xn
        w_sb = sb("w_sb", [P, W_COLS])
        c_sb = sb("c_sb", [P, C_COLS])
        ones = sb("ones", [P, P])
        fc1_sb = sb("fc1_sb", [BODY * BASIS, BODY, HID])
        fc2_sb = sb("fc2_sb", [HID, P])
        len_sb = sb("len_sb", [BODY * BASIS, (TURNS + 1) * QE])
        idx_sb = sb("idx_sb", [P, TILES + AHEAD * TQ], i32)
        idx_now = sb("idx_now", [P, SLOTS, TQ], i32)
        dst_sb = sb("dst_sb", [P, TILES + TQ], i32)
        dst_rel = sb("dst_rel", [P, TILES + TQ])
        ea_sb = sb("ea_sb", [P, TILES + TQ, NK])
        dq_sb = sb("dq_sb", [QUADS, QE], i32)
        q_min = sb("q_min", [QUADS, 1])
        q_max = sb("q_max", [QUADS, 1])
        q_span = sb("q_span", [QUADS, 1])
        diag = sb("diag", [QUADS, 2, QUADS])
        base_row = sb("base_row", [1, QUADS], i32)
        span_top = sb("span_top", [P, 1])
        rounds_sb = sb("rounds_sb", [P, 1], i32)
        h_sb = sb("h_sb", [HID, 2, QE])
        y_src = sb("y_src", [P, SLOTS, TQ, FEAT])
        prod = sb("prod", [P, 2, TQ, 2, FEAT])
        sel = sb("sel", [P, 2, TQ, NK, WIN])
        agg = sb("agg", [P, NK, NP])

        fc1_ps = [pb(f"fc1_ps{i}") for i in range(2)]
        w_ps = [pb(f"w_ps{i}") for i in range(2)]
        agg_ps = pb("agg_ps")
        self_ps = pb("self_ps")
        win_ps = pb("win_ps")

        s_x = [sem(f"s_x{i}") for i in range(len(BATCHES))]
        s_attr = sem("s_attr")
        s_nw = sem("s_nw")
        s_const = sem("s_const")
        s_fc = sem("s_fc")
        s_idx = sem("s_idx")
        s_dst = sem("s_dst")
        s_dq = sem("s_dq")
        s_ea = sem("s_ea")
        s_len = sem("s_len")
        s_ones = sem("s_ones")
        s_zero = sem("s_zero")
        s_chain = sem("s_chain")
        s_diag = sem("s_diag")
        s_win = sem("s_win")
        s_rounds = sem("s_rounds")
        s_var = sem("s_var")
        s_std = sem("s_std")
        s_xn = sem("s_xn")
        s_xt = sem("s_xt")
        s_ht = sem("s_ht")
        s_y = sem("s_y")
        s_ysb = sem("s_ysb")
        s_table = sem("s_table")
        s_self = sem("s_self")
        s_skip = sem("s_skip")
        s_wscaled = sem("s_wscaled")
        idx_staged = sem("idx_staged")
        y_free = sem("y_free")
        quads_begun = sem("quads_begun")
        gathered = [sem(f"gathered{j}") for j in range(SLOTS)]
        fc1_done = sem("fc1_done")
        silu_done = sem("silu_done")
        fc2_done = sem("fc2_done")
        sel_done = sem("sel_done")
        prod_a_done = sem("prod_a_done")
        prod_b_done = sem("prod_b_done")
        agg_done = sem("agg_done")
        summed = sem("summed")
        moved = sem("moved")
        s_o = sem("s_o")
        s_osb = sem("s_osb")
        s_out = sem("s_out")

        ident = c_sb[:, C_IDENT:C_IDENT + P]
        iota = c_sb[:, C_IOTA:C_IOTA + WIN]
        x_rows = x.rearrange("(c p) f -> p c f", p=P)
        y_rows = y_table.rearrange("(c p) f -> p c f", p=P)
        out_rows = out.rearrange("(c p) f -> p c f", p=P)

        block = ctx.enter_context(nc.Block())

        @block.sync
        def _(sp):
            for i, (c, n) in enumerate(BATCHES):
                sp.dma_start(x_sb[:, c:c + n, :], x_rows[:, c:c + n, :]).then_inc(s_x[i], 16)
                if i == 0:
                    sp.dma_start(c_sb[:, :], consts).then_inc(s_const, 16)
                    sp.dma_start(w_sb[:, :], node_w).then_inc(s_nw, 16)
                    sp.dma_start(attr_sb[:, :], attr).then_inc(s_attr, 16)
            sp.dma_start(fc1_sb[:, :, :], fc1_w).then_inc(s_fc, 16)
            sp.dma_start(fc2_sb[:, :], fc2_w).then_inc(s_fc, 16)
            sp.dma_start(idx_sb[:, :], src_idx).then_inc(s_idx, 16)
            sp.dma_start(ea_sb[:, :, :], edge_at).then_inc(s_ea, 16)
            sp.dma_start(len_sb[:, :], lengths).then_inc(s_len, 16)
            for g, (c, n) in enumerate(GROUPS):
                sp.wait_ge(s_ysb, g + 1)
                sp.dma_start(y_rows[:, c:c + n, :], y_sb[:, c:c + n, :]).then_inc(s_table, 16)
            for g, (c, n) in enumerate(GROUPS):
                sp.wait_ge(s_osb, g + 1)
                sp.dma_start(out_rows[:, c:c + n, :], x_sb[:, c:c + n, :]).then_inc(s_out, 16)
            sp.wait_ge(s_out, 16 * len(GROUPS))

        @block.gpsimd
        def _(pool):
            nc.gpsimd.memset(ones[:, :], 1.0).then_inc(s_ones, 1)
            nc.gpsimd.memset(agg[:, :, :], 0.0).then_inc(s_zero, 1)
            pool.wait_ge(s_rounds, 1)
            rounds = nc.gpsimd.value_load(rounds_sb[0:1, 0:1], min_val=1, max_val=NP)
            pool.wait_ge(s_table, 16 * len(GROUPS))
            with nc.gpsimd.Fori(0, rounds) as r:
                with nc.gpsimd.Fori(0, TURNS) as b:
                    for j in range(BODY):
                        step = r * QUADS + b * BODY + j
                        pool.wait_ge(idx_staged, step + 1)
                        pool.wait_ge(y_free, step + 1)
                        pool.sem_inc(quads_begun, 1)
                        for t in range(TQ):
                            pool.indirect_dma_start(
                                y_src[:, j % SLOTS, t, :], None, y_table[:, :],
                                bass.IndirectOffsetOnAxis(idx_now[:, j % SLOTS, t:t + 1], 0),
                            ).then_inc(gathered[j % SLOTS], 16)

        @block.scalar
        def _(act):
            act.dma_start(dq_sb[:, :], dst_quads).then_inc(s_dq, 16)
            act.dma_start(dst_sb[:, :], dst_tiles).then_inc(s_dst, 16)
            for i, (c, n) in enumerate(BATCHES):
                act.wait_ge(s_var, i + 1)
                nc.scalar.activation(std[:, c:c + n], var[:, c:c + n], ACT.Sqrt).then_inc(s_std, 1)
            act.wait_ge(s_attr, 16)
            ng = len(GROUPS)
            for g in range(ng + 1):
                if g < ng:
                    c, n = GROUPS[g]
                    act.wait_ge(s_xt, g + 1)
                    nc.scalar.activation(h_t[:, c:c + n, :], fc1_ps[g % 2][:, 0:n * P],
                                         ACT.Relu).then_inc(s_ht, 1)
                if g:
                    c, n = GROUPS[g - 1]
                    act.wait_ge(s_y, g)
                    for k in range(n):
                        last = nc.scalar.mul(y_sb[:, c + k, :], w_ps[(g - 1) % 2][:, k * P:(k + 1) * P],
                                             attr_sb[:, c + k:c + k + 1])
                    last.then_inc(s_ysb, 1)

            def stage(q_col, slot):
                nc.scalar.copy(idx_now[:, slot, :], idx_sb[:, q_col]).then_inc(idx_staged, 1)

            def silu(i):
                nc.scalar.activation(h_sb[:, i, :], fc1_ps[i][0:HID, :], ACT.Silu,
                                     scale=C_FC1).then_inc(silu_done, 1)

            act.wait_ge(s_idx, 16)
            for q in range(AHEAD):
                stage(slice(q * TQ, (q + 1) * TQ), q)
            act.wait_ge(fc1_done, 1)
            silu(0)
            act.wait_ge(s_rounds, 1)
            rounds = nc.scalar.value_load(rounds_sb[0:1, 0:1], min_val=1, max_val=NP)
            with nc.scalar.Fori(0, rounds) as r:
                with nc.scalar.Fori(0, TURNS) as b:
                    for j in range(BODY):
                        step = r * QUADS + b * BODY + j
                        act.wait_ge(y_free, step + AHEAD + 1)
                        stage(bass.ds((b * BODY + j + AHEAD) * TQ, TQ), (j + AHEAD) % SLOTS)
                        act.wait_ge(fc1_done, step + 2)
                        silu((j + 1) % 2)

        @block.vector
        def _(dve):
            links = [0]

            def link(ins):
                links[0] += 1
                ins.then_inc(s_chain, 1)
                dve.wait_ge(s_chain, links[0])

            dve.wait_ge(s_dq, 16)
            nc.vector.tensor_reduce(q_min[:, :], dq_sb[:, :], AX.X, ALU.min).then_inc(s_chain, 1)
            nc.vector.tensor_reduce(q_max[:, :], dq_sb[:, :], AX.X, ALU.max).then_inc(s_chain, 1)
            links[0] += 2
            dve.wait_ge(s_chain, links[0])
            link(nc.vector.tensor_tensor(q_span[:, :], q_max[:, :], q_min[:, :], ALU.subtract))
            dve.wait_ge(s_const, 16)
            nc.vector.tensor_scalar(diag[:, 0, :], ident[0:QUADS, 0:QUADS], q_min[:, 0:1], None, ALU.mult)
            nc.vector.tensor_scalar(diag[:, 1, :], ident[0:QUADS, 0:QUADS], q_span[:, 0:1], None,
                                    ALU.mult).then_inc(s_diag, 1)

            def normalise(i):
                c, n = BATCHES[i]
                cs = slice(c, c + n)
                dve.wait_ge(s_x[i], 16)
                for k in range(c, c + n):
                    last = nc.vector.bn_stats(stats[:, k, :], x_sb[:, k, :])
                link(last)
                m0, v0, m1, v1 = (stats[:, cs, k] for k in (1, 2, 4, 5))
                nc.vector.tensor_tensor(m_diff[:, cs], m0, m1, ALU.subtract)
                nc.vector.tensor_tensor(m_sum[:, cs], m0, m1, ALU.add)
                link(nc.vector.tensor_tensor(v_sum[:, cs], v0, v1, ALU.add))
                nc.vector.tensor_scalar(mean[:, cs], m_sum[:, cs], 0.5, None, ALU.mult)
                nc.vector.tensor_scalar(v_sum[:, cs], v_sum[:, cs], 1.0 / FEAT, LN_EPS, ALU.mult, ALU.add)
                link(nc.vector.scalar_tensor_tensor(m_sq[:, cs], m_diff[:, cs], 0.25, m_diff[:, cs],
                                                    ALU.mult, ALU.mult))
                nc.vector.tensor_tensor(var[:, cs], m_sq[:, cs], v_sum[:, cs], ALU.add).then_inc(s_var, 1)
                dve.wait_ge(s_std, i + 1)
                link(nc.vector.reciprocal(rstd[:, cs], std[:, cs]))
                for k in range(c, c + n):
                    nc.vector.tensor_scalar(xn[:, k, :], x_sb[:, k, :], mean[:, k:k + 1], rstd[:, k:k + 1],
                                            ALU.subtract, ALU.mult).then_inc(s_xn, 1)

            normalise(0)
            normalise(1)

            dve.wait_ge(s_win, 1)
            nc.vector.tensor_copy(base_row[:, :], win_ps[0:1, 0:QUADS])
            link(nc.vector.tensor_reduce(span_top[:, :], win_ps[:, QUADS:2 * QUADS], AX.X, ALU.max))
            nc.vector.tensor_scalar(rounds_sb[:, :], span_top[:, :], 1.0 / WIN, ROUND_UP,
                                    ALU.mult, ALU.add).then_inc(s_rounds, 1)

            normalise(2)
            normalise(3)

            dve.wait_ge(s_dst, 16)
            nc.vector.tensor_tensor(
                dst_rel[:, 0:TILES].rearrange("p (q t) -> p q t", t=TQ),
                dst_sb[:, 0:TILES].rearrange("p (q t) -> p q t", t=TQ),
                win_ps[:, 0:QUADS].unsqueeze(2).to_broadcast([P, QUADS, TQ]), ALU.subtract)
            link(nc.vector.tensor_tensor(dst_rel[:, TILES:], dst_sb[:, TILES:],
                                         win_ps[:, 0:1].to_broadcast([P, TQ]), ALU.subtract))
            link(nc.vector.tensor_scalar(dst_rel[:, TILES:], dst_rel[:, TILES:], float(WIN), None,
                                         ALU.subtract))
            dve.wait_ge(s_nw, 16)
            nc.vector.tensor_scalar(w_sb[:, W_SELF:W_AGG], w_sb[:, W_SELF:W_AGG], C_SELF, None,
                                    ALU.mult).then_inc(s_wscaled, 1)
            nc.vector.tensor_scalar(w_sb[:, W_AGG:W_DOT], w_sb[:, W_AGG:W_DOT], C_AGG, None, ALU.mult)
            for lo, hi, scale in ((0, 32, C_AGG), (32, 64, C_DOT), (64, 128, C_DOT)):
                last = nc.vector.tensor_scalar(w_sb[lo:hi, W_DOT:], w_sb[lo:hi, W_DOT:], scale, None,
                                               ALU.mult)
            last.then_inc(s_wscaled, 1)

            def build_sel(col, i):
                for t in range(TQ):
                    last = nc.vector.scalar_tensor_tensor(
                        sel[:, i, t, :, :],
                        iota.unsqueeze(1).to_broadcast([P, NK, WIN]),
                        dst_rel[:, bass.ds(col + t, 1)],
                        ea_sb[:, bass.ds(col + t, 1), :].rearrange("p o k -> p (o k)").unsqueeze(2)
                        .to_broadcast([P, NK, WIN]),
                        ALU.is_equal, ALU.mult)
                last.then_inc(sel_done, 1)

            dve.wait_ge(s_ea, 16)
            build_sel(0, 0)

            for g, (c, n) in enumerate(GROUPS):
                dve.wait_ge(s_self, g + 1)
                ps = (agg_ps, self_ps)[g % 2]
                for k in range(n):
                    last = nc.vector.scalar_tensor_tensor(
                        x_sb[:, c + k, :], ps[:, k * P:(k + 1) * P], attr_sb[:, c + k:c + k + 1],
                        x_sb[:, c + k, :], ALU.mult, ALU.add)
                last.then_inc(s_skip, 1)

            dve.sem_inc(y_free, SLOTS)
            dve.sem_inc(summed, 1)
            dve.wait_ge(s_zero, 1)
            rounds = nc.vector.value_load(rounds_sb[0:1, 0:1], min_val=1, max_val=NP)
            with nc.vector.Fori(0, rounds) as r:
                with nc.vector.Fori(0, TURNS) as b:
                    for j in range(BODY):
                        i = j % 2
                        quad = b * BODY + j
                        step = r * QUADS + quad
                        base = nc.vector.value_load(base_row[0:1, bass.ds(quad, 1)],
                                                    min_val=0, max_val=NP - WIN)
                        dve.wait_ge(fc2_done, step + 1)
                        use = (r * TURNS + b) * (BODY // SLOTS) + j // SLOTS + 1
                        dve.wait_ge(gathered[j % SLOTS], use * (16 * TQ))
                        w = w_ps[i][:, :].rearrange("p (t k u) -> p t k u", t=TQ, k=4)
                        y = y_src[:, j % SLOTS, :, :].rearrange("p t (k u) -> p t k u", k=4)
                        pr = prod[:, i, :, :, :].rearrange("p t a (k u) -> p t a k u", k=4)
                        nc.vector.tensor_tensor(
                            pr[:, :, :, 0, :], w[:, :, 0:2, :],
                            y[:, :, 0:1, :].to_broadcast([P, TQ, 2, MUL]), ALU.mult)
                        nc.vector.tensor_tensor(
                            pr[:, :, 0, 1:4, :], w[:, :, 2:3, :].to_broadcast([P, TQ, 3, MUL]),
                            y[:, :, 1:4, :], ALU.mult).then_inc(prod_a_done, 1)
                        last = nc.vector.tensor_tensor(
                            pr[:, :, 1, 1:4, :], w[:, :, 3:4, :].to_broadcast([P, TQ, 3, MUL]),
                            y[:, :, 1:4, :], ALU.mult)
                        last.then_inc(prod_b_done, 1)
                        build_sel((quad + 1) * TQ, (j + 1) % 2)
                        dve.wait_ge(prod_b_done, step + 1)
                        dve.sem_inc(y_free, 1)
                        dve.wait_ge(agg_done, step + 1)
                        dve.wait_ge(summed, step + 1)
                        here = agg[:, :, bass.ds(base, WIN)]
                        nc.vector.tensor_tensor(
                            here, here, agg_ps[:, 0:NK * WIN].rearrange("p (k n) -> p k n", k=NK),
                            ALU.add).then_inc(summed, 1)
                dve.wait_ge(sel_done, (r + 1) * QUADS + 1)
                nc.vector.tensor_scalar(dst_rel[:, :], dst_rel[:, :], float(WIN), None,
                                        ALU.subtract).then_inc(moved, 1)
                nc.vector.tensor_scalar(base_row[:, :], base_row[:, :], float(WIN), float(NP - WIN),
                                        ALU.add, ALU.min).then_inc(moved, 1)
                dve.wait_ge(moved, (r + 1) * 2)

            for g, (c, n) in enumerate(GROUPS):
                dve.wait_ge(s_o, g + 1)
                for k in range(n):
                    last = nc.vector.scalar_tensor_tensor(
                        x_sb[:, c + k, :], w_ps[g % 2][:, k * P:(k + 1) * P],
                        attr_sb[:, c + k:c + k + 1], x_sb[:, c + k, :], ALU.mult, ALU.add)
                last.then_inc(s_osb, 1)

        @block.tensor
        def _(pe):
            pe.wait_ge(s_ones, 1)
            pe.wait_ge(s_diag, 1)
            nc.tensor.matmul(win_ps[:, 0:2 * QUADS], ones[0:QUADS, :],
                             diag[:, :, :].rearrange("q a n -> q (a n)"),
                             start=True, stop=True).then_inc(s_win, 1)
            pe.wait_ge(s_const, 16)
            pe.wait_ge(s_nw, 16)
            ng = len(GROUPS)
            for g in range(ng + 1):
                if g < ng:
                    c, n = GROUPS[g]
                    if g >= 2:
                        pe.wait_ge(s_ht, g - 1)
                    for k in range(n):
                        pe.wait_ge(s_xn, c + k + 1)
                        last = nc.tensor.transpose(fc1_ps[g % 2][:, k * P:(k + 1) * P], xn[:, c + k, :],
                                                   ident)
                    last.then_inc(s_xt, 1)
                if g:
                    c, n = GROUPS[g - 1]
                    pe.wait_ge(s_ht, g)
                    if g >= 3:
                        pe.wait_ge(s_ysb, g - 2)
                    for k in range(n):
                        last = nc.tensor.matmul(w_ps[(g - 1) % 2][:, k * P:(k + 1) * P], h_t[:, c + k, :],
                                                w_sb[:, W_IN:W_IN + P], start=True, stop=True)
                    last.then_inc(s_y, 1)

            def fc1(col, group, i):
                nc.tensor.matmul(fc1_ps[i][0:HID, :], fc1_sb[:, group, :], len_sb[:, col],
                                 start=True, stop=True).then_inc(fc1_done, 1)

            def fc2(i):
                for t in range(TQ):
                    last = nc.tensor.matmul(w_ps[i][:, t * P:(t + 1) * P], h_sb[:, i, t * P:(t + 1) * P],
                                            fc2_sb[:, :], start=True, stop=True)
                last.then_inc(fc2_done, 1)

            pe.wait_ge(s_fc, 32)
            pe.wait_ge(s_len, 16)
            pe.wait_ge(s_ht, ng)
            fc1(slice(0, QE), 0, 0)
            fc1(slice(0, QE), 1, 1)
            pe.wait_ge(s_ysb, ng)
            pe.wait_ge(silu_done, 1)
            fc2(0)

            pe.wait_ge(s_wscaled, 1)
            for g, (c, n) in enumerate(GROUPS):
                if g >= 2:
                    pe.wait_ge(s_skip, g - 1)
                ps = (agg_ps, self_ps)[g % 2]
                for k in range(n):
                    last = nc.tensor.matmul(ps[:, k * P:(k + 1) * P], h_t[:, c + k, :],
                                            w_sb[:, W_SELF:W_SELF + P], start=True, stop=True)
                last.then_inc(s_self, 1)
            pe.wait_ge(s_skip, ng)

            pe.wait_ge(s_rounds, 1)
            rounds = nc.tensor.value_load(rounds_sb[0:1, 0:1], min_val=1, max_val=NP)
            with nc.tensor.Fori(0, rounds) as r:
                with nc.tensor.Fori(0, TURNS) as b:
                    for j in range(BODY):
                        i = j % 2
                        step = r * QUADS + b * BODY + j
                        pe.wait_ge(silu_done, step + 2)
                        fc2((j + 1) % 2)
                        fc1(bass.ds((b + (j + 2) // BODY) * QE, QE), (j + 2) % BODY, i)
                        pe.wait_ge(sel_done, step + 1)
                        pe.wait_ge(prod_a_done, step + 1)
                        for t in range(TQ):
                            nc.tensor.matmul(agg_ps[:, 0:WIN], prod[:, i, t, 0, :], sel[:, i, t, 0, :],
                                             start=(t == 0), stop=(t == TQ - 1))
                        pe.wait_ge(prod_b_done, step + 1)
                        for t in range(TQ):
                            last = nc.tensor.matmul(agg_ps[:, WIN:NK * WIN], prod[:, i, t, 1, :],
                                                    sel[:, i, t, 1:NK, :].rearrange("p k n -> p (k n)"),
                                                    start=(t == 0), stop=(t == TQ - 1))
                        last.then_inc(agg_done, 1)

            pe.wait_ge(s_wscaled, 2)
            pe.wait_ge(summed, rounds * QUADS + 1)
            for g, (c, n) in enumerate(GROUPS):
                if g >= 2:
                    pe.wait_ge(s_osb, g - 1)
                for k in range(n):
                    o = w_ps[g % 2][:, k * P:(k + 1) * P]
                    nodes = slice((c + k) * P, (c + k + 1) * P)
                    nc.tensor.matmul(o, agg[:, 0, nodes], w_sb[:, W_AGG:W_AGG + P], start=True, stop=False)
                    for d in range(3):
                        cols = o.rearrange("p (k u) -> p k u", k=4)[:, 0:d + 2:d + 1, :]
                        wd = w_sb[:, W_DOT + 64 * d:W_DOT + 64 * (d + 1)].rearrange("p (k u) -> p k u", k=2)
                        last = nc.tensor.matmul(cols, agg[:, 1 + d, nodes], wd, start=False, stop=(d == 2))
                last.then_inc(s_o, 1)


def kernel(x, src, dst, edge_attr_10, edge_attr_4, node_vec1, L0_gnn_W_sc0, L0_gnn_W_sc1,
           L0_gnn_W_l10, L0_gnn_W_l11, L0_gnn_W_l20, L0_gnn_W_l21, L0_gnn_W_fc1, L0_gnn_W_fc2):
    import numpy as np
    import concourse.bacc as bacc
    from concourse.bass_utils import run_bass_kernel_spmd

    f = np.float32

    def by_direction(a):
        v = a[:, MUL:].reshape(-1, MUL, 3).transpose(0, 2, 1).reshape(-1, 3 * MUL)
        return np.concatenate([a[:, :MUL], v], axis=1)

    def padded(a, rows):
        o = np.zeros((rows,) + a.shape[1:], a.dtype)
        o[:a.shape[0]] = a
        return o

    def blocks(w0, w1):
        o = np.zeros((FEAT, FEAT), f)
        for k, w in enumerate((w0, w1, w1, w1)):
            o[k * MUL:(k + 1) * MUL, k * MUL:(k + 1) * MUL] = w
        return o

    x, src, dst = np.asarray(x), np.asarray(src), np.asarray(dst)
    ea, lens = np.asarray(edge_attr_4), np.asarray(edge_attr_10)
    w20, w21 = np.asarray(L0_gnn_W_l20), np.asarray(L0_gnn_W_l21)
    E = QUADS * QE

    node_w = np.zeros((FEAT, W_COLS), f)
    node_w[:, W_IN:W_IN + P] = blocks(L0_gnn_W_l10, L0_gnn_W_l11)
    node_w[:, W_SELF:W_SELF + P] = blocks(L0_gnn_W_sc0, L0_gnn_W_sc1)
    node_w[:, W_AGG:W_AGG + P] = blocks(w20[:MUL], w21[MUL:])
    for d in range(3):
        c = W_DOT + 64 * d
        node_w[MUL * (d + 1):MUL * (d + 2), c:c + MUL] = w20[MUL:]
        node_w[:MUL, c + MUL:c + 2 * MUL] = w21[:MUL]
    consts = np.zeros((P, C_COLS), f)
    consts[:, C_IDENT:C_IDENT + P] = np.eye(P, dtype=f)
    consts[:, C_IOTA:C_IOTA + WIN] = np.arange(WIN, dtype=f)
    fc1_w = np.zeros((BODY, BASIS, BODY, HID), f)
    for j in range(BODY):
        fc1_w[j, :, j] = L0_gnn_W_fc1

    def tiles(a, extra):
        t = a.reshape((TILES, P) + a.shape[1:])
        t = t.transpose((1, 0) + tuple(range(2, t.ndim)))
        return np.concatenate([t, t[:, :extra]], axis=1)

    src_p = padded(src, E)
    dst_p = np.concatenate([dst, np.repeat(dst[-1:], E - EDGES)])
    len_p = padded(lens, E).reshape(TURNS, BODY, QE, BASIS).transpose(1, 3, 0, 2).reshape(
        BODY * BASIS, TURNS * QE)

    arrays = {
        "x": by_direction(padded(x, NP)),
        "attr": padded(np.asarray(node_vec1), NP).reshape(CHUNKS, P).T,
        "node_w": node_w,
        "consts": consts,
        "fc1_w": fc1_w.reshape(BODY * BASIS, BODY, HID),
        "fc2_w": np.asarray(L0_gnn_W_fc2),
        "src_idx": tiles(src_p, AHEAD * TQ),
        "dst_tiles": tiles(dst_p, TQ),
        "dst_quads": dst_p.reshape(QUADS, QE),
        "edge_at": tiles(padded(ea, E), TQ),
        "lengths": np.concatenate([len_p, len_p[:, :QE]], axis=1),
    }
    arrays = {f"{k}_dram": np.ascontiguousarray(a) for k, a in arrays.items()}
    nc = bacc.Bacc("TRN2", target_bir_lowering=False, num_devices=1)
    args = [nc.dram_tensor(k, a.shape, mybir.dt.from_np(a.dtype), kind="ExternalInput").ap()
            for k, a in arrays.items()]
    y_table = nc.dram_tensor("y_table", (NP, FEAT), mybir.dt.float32, kind="Internal").ap()
    out = nc.dram_tensor("out_dram", (NP, FEAT), mybir.dt.float32, kind="ExternalOutput").ap()
    edge_conv_program(nc, *args, y_table, out)
    o = run_bass_kernel_spmd(nc, [arrays], core_ids=[0]).results[0]["out_dram"][:NODES]
    v = o[:, MUL:].reshape(NODES, 3, MUL).transpose(0, 2, 1).reshape(NODES, 3 * MUL)
    return np.concatenate([o[:, :MUL], v], axis=1)
```

```python
import math
from contextlib import ExitStack

import concourse.bass as bass
from concourse import mybir

P = 128
NODES, FEAT, MUL = 3125, 128, 32
EDGES, BASIS, HID = 53125, 10, 100
CHUNKS = -(-NODES // P)
NP = CHUNKS * P
TQ = 4
QE = TQ * P
QUADS = -(-EDGES // QE)
BODY = 8
SLOTS = 4
TURNS = QUADS // BODY
TILES = QUADS * TQ
LEAD = 3
SLOTS_C = CHUNKS + LEAD
FLUSH_AT = (1, 4)
LAST_FLUSHED = 2 * TURNS - LEAD
WIN = 42
NK = 4
AHEAD = 2
LN_EPS = 1e-5
ROUND_UP = 0.51

assert QUADS % BODY == 0 and BODY % SLOTS == 0 and SLOTS % 2 == 0

C_SELF = math.sin(math.pi / 8) / math.sqrt(MUL)
C_AGG = (math.cos(math.pi / 8) / math.sqrt(2 * MUL) / math.sqrt(16.0)
         / math.sqrt(HID) / math.sqrt(MUL))
C_DOT = C_AGG / math.sqrt(3.0)
C_FC1 = 1.0 / math.sqrt(BASIS)

BATCHES = [(0, 4), (4, 8), (12, 8), (20, 5)]
GROUPS = [(c, min(4, CHUNKS - c)) for c in range(0, CHUNKS, 4)]

BATCH_OF = [next(i for i, (b, m) in enumerate(BATCHES) if b <= c < b + m) for c, _ in GROUPS]

W_IN, W_SELF, W_AGG, W_DOT = 0, 128, 256, 384
W_COLS = W_DOT + 3 * 64
C_IDENT, C_IOTA = 0, 128
C_DUE = C_IOTA + WIN
C_COLS = C_DUE + QUADS


def edge_conv_program(nc, x, attr, node_w, consts, fc1_w, fc2_w, src_idx, dst_tiles, dst_quads,
                      edge_at, lengths, y_table, out):
    f32, i32 = mybir.dt.float32, mybir.dt.int32
    ALU = mybir.AluOpType
    ACT = mybir.ActivationFunctionType
    AX = mybir.AxisListType

    ctx = ExitStack()
    with ctx:
        def sb(name, shape, dt=f32):
            return ctx.enter_context(nc.sbuf_tensor(name, shape, dt))

        def pb(name):
            return ctx.enter_context(nc.psum_tensor(name, [P, 512], f32))

        def sem(name):
            return ctx.enter_context(nc.semaphore(name))

        out_sb = sb("out_sb", [P, SLOTS_C, FEAT])
        x_sb = out_sb[:, LEAD:, :]
        attr_all = sb("attr_all", [P, SLOTS_C])
        attr_sb = attr_all[:, LEAD:]
        stats = sb("stats", [P, CHUNKS, 6])
        m_sum = sb("m_sum", [P, CHUNKS])
        m_diff = sb("m_diff", [P, CHUNKS])
        v_sum = sb("v_sum", [P, CHUNKS])
        m_sq = sb("m_sq", [P, CHUNKS])
        shift = sb("shift", [P, CHUNKS])
        var = sb("var", [P, CHUNKS])
        std = sb("std", [P, CHUNKS])
        rstd = sb("rstd", [P, CHUNKS])
        xn = sb("xn", [P, CHUNKS, FEAT])
        h_t = sb("h_t", [P, CHUNKS, P])
        y_sb = xn
        w_sb = sb("w_sb", [P, W_COLS])
        c_sb = sb("c_sb", [P, C_COLS])
        ones = sb("ones", [P, P])
        fc1_sb = sb("fc1_sb", [BODY * BASIS, BODY, HID])
        fc2_sb = sb("fc2_sb", [HID, P])
        len_sb = sb("len_sb", [BODY * BASIS, (TURNS + 1) * QE])
        idx_sb = sb("idx_sb", [P, TILES + AHEAD * TQ], i32)
        idx_now = sb("idx_now", [P, SLOTS, TQ], i32)
        dst_sb = sb("dst_sb", [P, TILES + TQ], i32)
        dst_rel = sb("dst_rel", [P, TILES + TQ])
        ea_sb = sb("ea_sb", [P, TILES + TQ, NK])
        dq_sb = sb("dq_sb", [QUADS, QE], i32)
        q_min = sb("q_min", [QUADS, 1])
        q_max = sb("q_max", [QUADS, 1])
        q_span = sb("q_span", [QUADS, 1])
        diag = sb("diag", [QUADS, 2, QUADS])
        base_row = sb("base_row", [1, 1 + QUADS], i32)
        span_top = sb("span_top", [P, 1])
        rounds_sb = sb("rounds_sb", [P, 1], i32)
        slack = sb("slack", [P, QUADS])
        slack_min = sb("slack_min", [P, 1])
        one_round = sb("one_round", [P, 1])
        complete = sb("complete", [P, 1])
        again = sb("again", [P, 2], i32)
        h_sb = sb("h_sb", [HID, 2, QE])
        y_src = sb("y_src", [P, SLOTS, TQ, FEAT])
        prod = sb("prod", [P, 2, TQ, 2, FEAT])
        sel = sb("sel", [P, 2, TQ, NK, WIN])
        agg = sb("agg", [P, NK, SLOTS_C * P])
        blank = sb("blank", [P, 1, 1])
        stage_sb = sb("stage_sb", [P, NK, P])

        fc1_ps = [pb(f"fc1_ps{i}") for i in range(2)]
        w_ps = [pb(f"w_ps{i}") for i in range(2)]
        agg_ps = [pb(f"agg_ps{i}") for i in range(2)]
        win_ps = pb("win_ps")
        flush_ps = pb("flush_ps")

        s_x = [sem(f"s_x{i}") for i in range(len(BATCHES))]
        s_attr = sem("s_attr")
        s_nw = sem("s_nw")
        s_const = sem("s_const")
        s_fc = sem("s_fc")
        s_idx = sem("s_idx")
        s_dst = sem("s_dst")
        s_dq = sem("s_dq")
        s_ea = sem("s_ea")
        s_len = sem("s_len")
        s_ones = sem("s_ones")
        s_zero = sem("s_zero")
        s_chain = sem("s_chain")
        s_diag = sem("s_diag")
        s_win = sem("s_win")
        s_rounds = sem("s_rounds")
        s_var = sem("s_var")
        s_std = sem("s_std")
        s_rstd = sem("s_rstd")
        s_xn = sem("s_xn")
        s_xt = sem("s_xt")
        s_ht = sem("s_ht")
        s_y = sem("s_y")
        s_ysb = sem("s_ysb")
        s_table = sem("s_table")
        s_self = sem("s_self")
        s_skip = sem("s_skip")
        s_wscaled = sem("s_wscaled")
        idx_staged = sem("idx_staged")
        y_free = sem("y_free")
        quads_begun = sem("quads_begun")
        gathered = [sem(f"gathered{j}") for j in range(SLOTS)]
        fc1_done = sem("fc1_done")
        silu_done = sem("silu_done")
        fc2_done = sem("fc2_done")
        sel_done = sem("sel_done")
        prod_a_done = sem("prod_a_done")
        prod_b_done = sem("prod_b_done")
        agg_done = sem("agg_done")
        summed = sem("summed")
        moved = sem("moved")
        s_blank = sem("s_blank")
        s_again = sem("s_again")
        staged = sem("staged")
        stages = sem("stages")
        cleared = sem("cleared")
        mapped = sem("mapped")
        flushed = sem("flushed")
        s_out = sem("s_out")
        all_stored = sem("all_stored")

        ident = c_sb[:, C_IDENT:C_IDENT + P]
        iota = c_sb[:, C_IOTA:C_IOTA + WIN]
        x_rows = x.rearrange("(c p) f -> p c f", p=P)
        y_rows = y_table.rearrange("(c p) f -> p c f", p=P)
        out_rows = out.rearrange("(c p) f -> p c f", p=P)

        def last_chunks(c):
            return nc.s_assert_within(
                c, LEAD, SLOTS_C - 1,
                skip_runtime_bounds_check_because="first + count is SLOTS_C, as both come from one flag")

        block = ctx.enter_context(nc.Block())

        @block.sync
        def _(sp):
            def load_x(i):
                c, n = BATCHES[i]
                sp.dma_start(x_sb[:, c:c + n, :], x_rows[:, c:c + n, :]).then_inc(s_x[i], 16)

            sp.sem_inc(s_out, 16)
            load_x(0)
            load_x(1)
            sp.dma_start(c_sb[:, :], consts).then_inc(s_const, 16)
            load_x(2)
            load_x(3)
            sp.dma_start(dq_sb[:, :], dst_quads).then_inc(s_dq, 16)
            sp.dma_start(fc1_sb[:, :, :], fc1_w).then_inc(s_fc, 16)
            sp.dma_start(ea_sb[:, :, :], edge_at).then_inc(s_ea, 16)
            sp.dma_start(len_sb[:, :], lengths).then_inc(s_len, 16)
            for g, (c, n) in enumerate(GROUPS):
                sp.wait_ge(s_ysb, g + 1)
                sp.dma_start(y_rows[:, c:c + n, :], y_sb[:, c:c + n, :]).then_inc(s_table, 16)
            sp.wait_ge(s_again, 2)
            rounds = nc.sync.value_load(rounds_sb[0:1, 0:1], min_val=1, max_val=NP)
            first = nc.sync.value_load(again[0:1, 0:1], min_val=LEAD, max_val=LEAD + LAST_FLUSHED)
            count = nc.sync.value_load(again[0:1, 1:2], min_val=CHUNKS - LAST_FLUSHED, max_val=CHUNKS)
            with nc.sync.Fori(0, rounds) as r:
                with nc.sync.Fori(0, TURNS) as b:
                    turn = r * TURNS + b
                    sp.wait_ge(flushed, turn * 2 + 3)
                    sp.wait_ge(s_out, turn * 16 + 16)
                    sp.dma_start(out_rows[:, bass.ds(b * 2, 2), :],
                                 out_sb[:, bass.ds(b * 2, 2), :]).then_inc(s_out, 16)
            stores = rounds * TURNS + 1
            with nc.sync.Fori(0, count) as k:
                sp.wait_ge(flushed, rounds * (TURNS * 2) + k + 2)
                sp.wait_ge(s_out, stores * 16 + k * 16)
                c = last_chunks(first + k)
                sp.dma_start(out_rows[:, bass.ds(c, 1), :],
                             out_sb[:, bass.ds(c, 1), :]).then_inc(s_out, 16)
            sp.wait_ge(s_out, stores * 16 + count * 16)
            sp.sem_inc(all_stored, 1)

        @block.gpsimd
        def _(pool):
            nc.gpsimd.memset(ones[:, :], 1.0).then_inc(s_ones, 1)
            nc.gpsimd.memset(blank[:, :, :], 0.0).then_inc(s_blank, 1)
            nc.gpsimd.memset(out_sb[:, 0:LEAD, :], 0.0).then_inc(s_blank, 1)
            nc.gpsimd.memset(agg[:, :, :], 0.0).then_inc(s_zero, 1)
            pool.wait_ge(s_rounds, 1)
            rounds = nc.gpsimd.value_load(rounds_sb[0:1, 0:1], min_val=1, max_val=NP)
            pool.wait_ge(s_table, 16 * len(GROUPS))
            with nc.gpsimd.Fori(0, rounds) as r:
                with nc.gpsimd.Fori(0, TURNS) as b:
                    for j in range(BODY):
                        step = r * QUADS + b * BODY + j
                        pool.wait_ge(idx_staged, step + 1)
                        pool.wait_ge(y_free, step + 1)
                        pool.sem_inc(quads_begun, 1)
                        for t in range(TQ):
                            pool.indirect_dma_start(
                                y_src[:, j % SLOTS, t, :], None, y_table[:, :],
                                bass.IndirectOffsetOnAxis(idx_now[:, j % SLOTS, t:t + 1], 0),
                            ).then_inc(gathered[j % SLOTS], 16)

        @block.scalar
        def _(act):
            act.dma_start(w_sb[:, :], node_w).then_inc(s_nw, 16)
            act.dma_start(attr_all[:, :], attr).then_inc(s_attr, 16)
            act.dma_start(fc2_sb[:, :], fc2_w).then_inc(s_fc, 16)
            act.dma_start(idx_sb[:, :], src_idx).then_inc(s_idx, 16)
            act.dma_start(dst_sb[:, :], dst_tiles).then_inc(s_dst, 16)

            def deviations(i):
                c, n = BATCHES[i]
                act.wait_ge(s_var, i + 1)
                nc.scalar.activation(std[:, c:c + n], var[:, c:c + n], ACT.Sqrt).then_inc(s_std, 1)

            def normalise(g):
                c, n = GROUPS[g]
                act.wait_ge(s_rstd, BATCH_OF[g] + 1)
                for k in range(c, c + n):
                    nc.scalar.activation(xn[:, k, :], x_sb[:, k, :], ACT.Identity, bias=shift[:, k:k + 1],
                                         scale=rstd[:, k:k + 1]).then_inc(s_xn, 1)

            def relu(g):
                c, n = GROUPS[g]
                act.wait_ge(s_xt, g + 1)
                nc.scalar.activation(h_t[:, c:c + n, :], fc1_ps[g % 2][:, 0:n * P],
                                     ACT.Relu).then_inc(s_ht, 1)

            for g in range(len(GROUPS) + 2):
                if g < len(GROUPS):
                    if g == 0 or BATCH_OF[g] != BATCH_OF[g - 1]:
                        deviations(BATCH_OF[g])
                    normalise(g)
                if g >= 2:
                    relu(g - 2)

            def stage(q_col, slot):
                nc.scalar.copy(idx_now[:, slot, :], idx_sb[:, q_col]).then_inc(idx_staged, 1)

            def silu(i):
                nc.scalar.activation(h_sb[:, i, :], fc1_ps[i][0:HID, :], ACT.Silu,
                                     scale=C_FC1).then_inc(silu_done, 1)

            act.wait_ge(s_idx, 16)
            for q in range(AHEAD):
                stage(slice(q * TQ, (q + 1) * TQ), q)
            act.wait_ge(fc1_done, 1)
            silu(0)
            act.wait_ge(s_rounds, 1)
            rounds = nc.scalar.value_load(rounds_sb[0:1, 0:1], min_val=1, max_val=NP)
            with nc.scalar.Fori(0, rounds) as r:
                with nc.scalar.Fori(0, TURNS) as b:
                    for j in range(BODY):
                        step = r * QUADS + b * BODY + j
                        act.wait_ge(y_free, step + AHEAD + 1)
                        stage(bass.ds((b * BODY + j + AHEAD) * TQ, TQ), (j + AHEAD) % SLOTS)
                        act.wait_ge(fc1_done, step + 2)
                        silu((j + 1) % 2)

        @block.vector
        def _(dve):
            links = [0]

            def link(ins):
                links[0] += 1
                ins.then_inc(s_chain, 1)
                dve.wait_ge(s_chain, links[0])

            def statistics(i):
                c, n = BATCHES[i]
                cs = slice(c, c + n)
                dve.wait_ge(s_x[i], 16)
                for k in range(c, c + n):
                    last = nc.vector.bn_stats(stats[:, k, :], x_sb[:, k, :])
                link(last)
                m0, v0, m1, v1 = (stats[:, cs, k] for k in (1, 2, 4, 5))
                nc.vector.tensor_tensor(m_sum[:, cs], m0, m1, ALU.add)
                nc.vector.tensor_tensor(m_diff[:, cs], m0, m1, ALU.subtract)
                link(nc.vector.tensor_tensor(v_sum[:, cs], v0, v1, ALU.add))
                nc.vector.tensor_scalar(v_sum[:, cs], v_sum[:, cs], 1.0 / FEAT, LN_EPS, ALU.mult, ALU.add)
                link(nc.vector.scalar_tensor_tensor(m_sq[:, cs], m_diff[:, cs], 0.25, m_diff[:, cs],
                                                    ALU.mult, ALU.mult))
                nc.vector.tensor_tensor(var[:, cs], m_sq[:, cs], v_sum[:, cs], ALU.add).then_inc(s_var, 1)

            def scales(i):
                c, n = BATCHES[i]
                cs = slice(c, c + n)
                dve.wait_ge(s_std, i + 1)
                link(nc.vector.reciprocal(rstd[:, cs], std[:, cs]))
                nc.vector.scalar_tensor_tensor(shift[:, cs], m_sum[:, cs], -0.5, rstd[:, cs],
                                               ALU.mult, ALU.mult).then_inc(s_rstd, 1)

            def table(g):
                c, n = GROUPS[g]
                dve.wait_ge(s_y, g + 1)
                nc.vector.tensor_tensor(
                    y_sb[:, c:c + n, :], w_ps[g % 2][:, 0:n * P].rearrange("p (c f) -> p c f", f=FEAT),
                    attr_sb[:, c:c + n].unsqueeze(2).to_broadcast([P, n, FEAT]), ALU.mult).then_inc(s_ysb, 1)

            dve.sem_inc(y_free, SLOTS)
            dve.sem_inc(summed, 1)
            statistics(0)
            scales(0)
            statistics(1)
            scales(1)
            statistics(2)
            scales(2)
            statistics(3)
            scales(3)

            dve.wait_ge(s_dq, 16)
            nc.vector.tensor_reduce(q_min[:, :], dq_sb[:, :], AX.X, ALU.min)
            link(nc.vector.tensor_reduce(q_max[:, :], dq_sb[:, :], AX.X, ALU.max))
            link(nc.vector.tensor_tensor(q_span[:, :], q_max[:, :], q_min[:, :], ALU.subtract))
            dve.wait_ge(s_const, 16)
            for a, ends in enumerate((q_min, q_span)):
                last = nc.vector.tensor_scalar(diag[:, a, :], ident[0:QUADS, 0:QUADS], ends[:, 0:1], None,
                                               ALU.mult)
            last.then_inc(s_diag, 1)

            dve.wait_ge(s_attr, 16)
            for g in range(len(GROUPS)):
                table(g)

            dve.wait_ge(s_win, 1)
            nc.vector.memset(base_row[:, 0:1], 0)
            nc.vector.tensor_scalar(base_row[:, 1:], win_ps[0:1, 0:QUADS], float(LEAD * P), None, ALU.add)
            nc.vector.tensor_tensor(slack[:, :], win_ps[:, 0:QUADS], c_sb[:, C_DUE:C_DUE + QUADS],
                                    ALU.subtract)
            link(nc.vector.tensor_reduce(span_top[:, :], win_ps[:, QUADS:2 * QUADS], AX.X, ALU.max))
            nc.vector.tensor_scalar(rounds_sb[:, :], span_top[:, :], 1.0 / WIN, ROUND_UP,
                                    ALU.mult, ALU.add).then_inc(s_rounds, 1)
            nc.vector.tensor_scalar(one_round[:, :], span_top[:, :], float(WIN), float(LAST_FLUSHED),
                                    ALU.is_lt, ALU.mult)
            link(nc.vector.tensor_reduce(slack_min[:, :], slack[:, :], AX.X, ALU.min))
            link(nc.vector.scalar_tensor_tensor(complete[:, :], slack_min[:, :], 0.0, one_round[:, :],
                                                ALU.is_ge, ALU.mult))
            nc.vector.tensor_scalar(again[:, 0:1], complete[:, :], float(LEAD), None,
                                    ALU.add).then_inc(s_again, 1)
            nc.vector.tensor_scalar(again[:, 1:2], complete[:, :], -1.0, float(CHUNKS), ALU.mult,
                                    ALU.add).then_inc(s_again, 1)

            dve.wait_ge(s_dst, 16)
            nc.vector.tensor_tensor(
                dst_rel[:, 0:TILES].rearrange("p (q t) -> p q t", t=TQ),
                dst_sb[:, 0:TILES].rearrange("p (q t) -> p q t", t=TQ),
                win_ps[:, 0:QUADS].unsqueeze(2).to_broadcast([P, QUADS, TQ]), ALU.subtract)
            link(nc.vector.tensor_tensor(dst_rel[:, TILES:], dst_sb[:, TILES:],
                                         win_ps[:, 0:1].to_broadcast([P, TQ]), ALU.subtract))
            link(nc.vector.tensor_scalar(dst_rel[:, TILES:], dst_rel[:, TILES:], float(WIN), None,
                                         ALU.subtract))
            dve.wait_ge(s_nw, 16)
            nc.vector.tensor_scalar(w_sb[:, W_SELF:W_AGG], w_sb[:, W_SELF:W_AGG], C_SELF, None,
                                    ALU.mult).then_inc(s_wscaled, 1)
            nc.vector.tensor_scalar(w_sb[:, W_AGG:W_DOT], w_sb[:, W_AGG:W_DOT], C_AGG, None, ALU.mult)
            for lo, hi, scale in ((0, 32, C_AGG), (32, 64, C_DOT), (64, 128, C_DOT)):
                last = nc.vector.tensor_scalar(w_sb[lo:hi, W_DOT:], w_sb[lo:hi, W_DOT:], scale, None,
                                               ALU.mult)
            last.then_inc(s_wscaled, 1)

            def build_sel(col, i):
                for t in range(TQ):
                    last = nc.vector.scalar_tensor_tensor(
                        sel[:, i, t, :, :],
                        iota.unsqueeze(1).to_broadcast([P, NK, WIN]),
                        dst_rel[:, bass.ds(col + t, 1)],
                        ea_sb[:, bass.ds(col + t, 1), :].rearrange("p o k -> p (o k)").unsqueeze(2)
                        .to_broadcast([P, NK, WIN]),
                        ALU.is_equal, ALU.mult)
                last.then_inc(sel_done, 1)

            dve.wait_ge(s_ea, 16)
            build_sel(0, 0)

            for g, (c, n) in enumerate(GROUPS):
                dve.wait_ge(s_self, g + 1)
                ps = agg_ps[g % 2]
                for k in range(n):
                    last = nc.vector.scalar_tensor_tensor(
                        x_sb[:, c + k, :], ps[:, k * P:(k + 1) * P], attr_sb[:, c + k:c + k + 1],
                        x_sb[:, c + k, :], ALU.mult, ALU.add)
                last.then_inc(s_skip, 1)

            dve.wait_ge(s_skip, len(GROUPS))
            nc.vector.memset(agg_ps[1][:, 0:NK * WIN], 0.0).then_inc(agg_done, 1)
            dve.wait_ge(s_zero, 1)

            def add_sums(base, i, step):
                dve.wait_ge(agg_done, step + 1)
                dve.wait_ge(summed, step + 1)
                here = agg[:, :, bass.ds(base, WIN)]
                nc.vector.tensor_tensor(
                    here, here, agg_ps[i][:, 0:NK * WIN].rearrange("p (k n) -> p k n", k=NK),
                    ALU.add).then_inc(summed, 1)


            def stage(c, n, adds):
                dve.wait_ge(mapped, n)
                dve.wait_ge(summed, adds)
                dve.sem_inc(stages, 1)
                nc.vector.tensor_copy(stage_sb[:, :, :], agg[:, :, bass.ds(c * P, P)]).then_inc(staged, 1)
                dve.wait_ge(staged, n)
                dve.sem_inc(stages, 1)
                nc.vector.tensor_copy(agg[:, :, bass.ds(c * P, P)],
                                      blank[:, :, :].to_broadcast([P, NK, P])).then_inc(cleared, 1)
                dve.wait_ge(cleared, n)

            def to_output(c, n, turn):
                dve.wait_ge(mapped, n + 1)
                dve.wait_ge(flushed, n)
                dve.wait_ge(s_out, turn * 16 + 16)
                nc.vector.scalar_tensor_tensor(
                    out_sb[:, bass.ds(c, 1), :].rearrange("p o f -> p (o f)"), flush_ps[:, 0:P],
                    attr_all[:, bass.ds(c, 1)], out_sb[:, bass.ds(c, 1), :].rearrange("p o f -> p (o f)"),
                    ALU.mult, ALU.add).then_inc(flushed, 1)

            dve.sem_inc(mapped, 1)
            dve.sem_inc(flushed, 1)
            dve.wait_ge(s_blank, 2)
            rounds = nc.vector.value_load(rounds_sb[0:1, 0:1], min_val=1, max_val=NP)
            first = nc.vector.value_load(again[0:1, 0:1], min_val=LEAD, max_val=LEAD + LAST_FLUSHED)
            count = nc.vector.value_load(again[0:1, 1:2], min_val=CHUNKS - LAST_FLUSHED, max_val=CHUNKS)
            with nc.vector.Fori(0, rounds) as r:
                with nc.vector.Fori(0, TURNS) as b:
                    turn = r * TURNS + b
                    for j in range(BODY):
                        i = j % 2
                        quad = b * BODY + j
                        step = r * QUADS + quad
                        base = nc.vector.value_load(base_row[0:1, bass.ds(quad, 1)],
                                                    min_val=0, max_val=SLOTS_C * P - WIN)
                        dve.wait_ge(fc2_done, step + 1)
                        use = turn * (BODY // SLOTS) + j // SLOTS + 1
                        dve.wait_ge(gathered[j % SLOTS], use * (16 * TQ))
                        w = w_ps[i][:, :].rearrange("p (t k u) -> p t k u", t=TQ, k=4)
                        y = y_src[:, j % SLOTS, :, :].rearrange("p t (k u) -> p t k u", k=4)
                        pr = prod[:, i, :, :, :].rearrange("p t a (k u) -> p t a k u", k=4)
                        nc.vector.tensor_tensor(
                            pr[:, :, :, 0, :], w[:, :, 0:2, :],
                            y[:, :, 0:1, :].to_broadcast([P, TQ, 2, MUL]), ALU.mult)
                        nc.vector.tensor_tensor(
                            pr[:, :, 0, 1:4, :], w[:, :, 2:3, :].to_broadcast([P, TQ, 3, MUL]),
                            y[:, :, 1:4, :], ALU.mult).then_inc(prod_a_done, 1)
                        nc.vector.tensor_tensor(
                            pr[:, :, 1, 1:4, :], w[:, :, 3:4, :].to_broadcast([P, TQ, 3, MUL]),
                            y[:, :, 1:4, :], ALU.mult).then_inc(prod_b_done, 1)
                        add_sums(base, 1 - i, step)
                        build_sel((quad + 1) * TQ, (j + 1) % 2)
                        dve.wait_ge(prod_b_done, step + 1)
                        dve.sem_inc(y_free, 1)
                        for k, at in enumerate(FLUSH_AT):
                            n = turn * 2 + k + 1
                            if j == at:
                                stage(b * 2 + k, n, step + 2)
                            if j == at + 2:
                                to_output(b * 2 + k, n, turn)
                dve.wait_ge(sel_done, (r + 1) * QUADS + 1)
                nc.vector.tensor_scalar(dst_rel[:, :], dst_rel[:, :], float(WIN), None,
                                        ALU.subtract).then_inc(moved, 1)
                nc.vector.tensor_copy(base_row[:, 0:1], base_row[:, QUADS:]).then_inc(moved, 1)
                dve.wait_ge(moved, r * 3 + 2)
                nc.vector.tensor_scalar(base_row[:, 1:], base_row[:, 1:], float(WIN), float(SLOTS_C * P - WIN),
                                        ALU.add, ALU.min).then_inc(moved, 1)
                dve.wait_ge(moved, r * 3 + 3)
            base = nc.vector.value_load(base_row[0:1, 0:1], min_val=0, max_val=SLOTS_C * P - WIN)
            add_sums(base, (QUADS - 1) % 2, rounds * QUADS)

            with nc.vector.Fori(0, count) as k:
                n = rounds * (TURNS * 2) + k + 1
                c = last_chunks(first + k)
                stage(c, n, rounds * QUADS + 2)
                to_output(c, n, rounds * TURNS)

        @block.tensor
        def _(pe):
            pe.wait_ge(s_const, 16)
            pe.wait_ge(s_nw, 16)
            ng = len(GROUPS)
            for g in range(ng + 1):
                if g < ng:
                    c, n = GROUPS[g]
                    if g >= 2:
                        pe.wait_ge(s_ht, g - 1)
                    for k in range(n):
                        pe.wait_ge(s_xn, c + k + 1)
                        last = nc.tensor.transpose(fc1_ps[g % 2][:, k * P:(k + 1) * P], xn[:, c + k, :],
                                                   ident)
                    last.then_inc(s_xt, 1)
                if g:
                    c, n = GROUPS[g - 1]
                    pe.wait_ge(s_ht, g)
                    if g >= 3:
                        pe.wait_ge(s_ysb, g - 2)
                    for k in range(n):
                        last = nc.tensor.matmul(w_ps[(g - 1) % 2][:, k * P:(k + 1) * P], h_t[:, c + k, :],
                                                w_sb[:, W_IN:W_IN + P], start=True, stop=True)
                    last.then_inc(s_y, 1)

            pe.wait_ge(s_ones, 1)
            pe.wait_ge(s_diag, 1)
            nc.tensor.matmul(win_ps[:, 0:2 * QUADS], ones[0:QUADS, :],
                             diag[:, :, :].rearrange("q a n -> q (a n)"),
                             start=True, stop=True).then_inc(s_win, 1)
            def fc1(col, group, i):
                nc.tensor.matmul(fc1_ps[i][0:HID, :], fc1_sb[:, group, :], len_sb[:, col],
                                 start=True, stop=True).then_inc(fc1_done, 1)

            def fc2(i):
                for t in range(TQ):
                    last = nc.tensor.matmul(w_ps[i][:, t * P:(t + 1) * P], h_sb[:, i, t * P:(t + 1) * P],
                                            fc2_sb[:, :], start=True, stop=True)
                last.then_inc(fc2_done, 1)

            pe.wait_ge(s_fc, 32)
            pe.wait_ge(s_len, 16)
            pe.wait_ge(s_ht, ng)
            fc1(slice(0, QE), 0, 0)
            fc1(slice(0, QE), 1, 1)
            pe.wait_ge(s_ysb, ng)
            pe.wait_ge(silu_done, 1)
            fc2(0)

            pe.wait_ge(s_wscaled, 1)
            for g, (c, n) in enumerate(GROUPS):
                if g >= 2:
                    pe.wait_ge(s_skip, g - 1)
                ps = agg_ps[g % 2]
                for k in range(n):
                    last = nc.tensor.matmul(ps[:, k * P:(k + 1) * P], h_t[:, c + k, :],
                                            w_sb[:, W_SELF:W_SELF + P], start=True, stop=True)
                last.then_inc(s_self, 1)
            pe.wait_ge(s_skip, ng)

            def linear(n):
                pe.wait_ge(staged, n)
                pe.wait_ge(flushed, n)
                o = flush_ps[:, 0:P]
                nc.tensor.matmul(o, stage_sb[:, 0, :], w_sb[:, W_AGG:W_AGG + P], start=True, stop=False)
                for d in range(3):
                    cols = o.rearrange("p (k u) -> p k u", k=4)[:, 0:d + 2:d + 1, :]
                    wd = w_sb[:, W_DOT + 64 * d:W_DOT + 64 * (d + 1)].rearrange("p (k u) -> p k u", k=2)
                    last = nc.tensor.matmul(cols, stage_sb[:, 1 + d, :], wd, start=False, stop=(d == 2))
                last.then_inc(mapped, 1)

            pe.wait_ge(s_wscaled, 2)
            pe.wait_ge(s_again, 2)
            rounds = nc.tensor.value_load(rounds_sb[0:1, 0:1], min_val=1, max_val=NP)
            count = nc.tensor.value_load(again[0:1, 1:2], min_val=CHUNKS - LAST_FLUSHED, max_val=CHUNKS)
            with nc.tensor.Fori(0, rounds) as r:
                with nc.tensor.Fori(0, TURNS) as b:
                    for j in range(BODY):
                        i = j % 2
                        step = r * QUADS + b * BODY + j
                        pe.wait_ge(silu_done, step + 2)
                        fc2((j + 1) % 2)
                        fc1(bass.ds((b + (j + 2) // BODY) * QE, QE), (j + 2) % BODY, i)
                        pe.wait_ge(sel_done, step + 1)
                        pe.wait_ge(prod_a_done, step + 1)
                        for t in range(TQ):
                            nc.tensor.matmul(agg_ps[i][:, 0:WIN], prod[:, i, t, 0, :], sel[:, i, t, 0, :],
                                             start=(t == 0), stop=(t == TQ - 1))
                        pe.wait_ge(prod_b_done, step + 1)
                        for t in range(TQ):
                            last = nc.tensor.matmul(agg_ps[i][:, WIN:NK * WIN], prod[:, i, t, 1, :],
                                                    sel[:, i, t, 1:NK, :].rearrange("p k n -> p (k n)"),
                                                    start=(t == 0), stop=(t == TQ - 1))
                        last.then_inc(agg_done, 1)
                        for k, at in enumerate(FLUSH_AT):
                            if j == at + 1:
                                linear((r * TURNS + b) * 2 + k + 1)
            with nc.tensor.Fori(0, count) as k:
                linear(rounds * (TURNS * 2) + k + 1)


def kernel(x, src, dst, edge_attr_10, edge_attr_4, node_vec1, L0_gnn_W_sc0, L0_gnn_W_sc1,
           L0_gnn_W_l10, L0_gnn_W_l11, L0_gnn_W_l20, L0_gnn_W_l21, L0_gnn_W_fc1, L0_gnn_W_fc2):
    import numpy as np
    import concourse.bacc as bacc
    from concourse.bass_utils import run_bass_kernel_spmd

    f = np.float32

    def by_direction(a):
        v = a[:, MUL:].reshape(-1, MUL, 3).transpose(0, 2, 1).reshape(-1, 3 * MUL)
        return np.concatenate([a[:, :MUL], v], axis=1)

    def padded(a, rows):
        o = np.zeros((rows,) + a.shape[1:], a.dtype)
        o[:a.shape[0]] = a
        return o

    def blocks(w0, w1):
        o = np.zeros((FEAT, FEAT), f)
        for k, w in enumerate((w0, w1, w1, w1)):
            o[k * MUL:(k + 1) * MUL, k * MUL:(k + 1) * MUL] = w
        return o

    x, src, dst = np.asarray(x), np.asarray(src), np.asarray(dst)
    ea, lens = np.asarray(edge_attr_4), np.asarray(edge_attr_10)
    w20, w21 = np.asarray(L0_gnn_W_l20), np.asarray(L0_gnn_W_l21)
    E = QUADS * QE

    node_w = np.zeros((FEAT, W_COLS), f)
    node_w[:, W_IN:W_IN + P] = blocks(L0_gnn_W_l10, L0_gnn_W_l11)
    node_w[:, W_SELF:W_SELF + P] = blocks(L0_gnn_W_sc0, L0_gnn_W_sc1)
    node_w[:, W_AGG:W_AGG + P] = blocks(w20[:MUL], w21[MUL:])
    for d in range(3):
        c = W_DOT + 64 * d
        node_w[MUL * (d + 1):MUL * (d + 2), c:c + MUL] = w20[MUL:]
        node_w[:MUL, c + MUL:c + 2 * MUL] = w21[:MUL]
    consts = np.zeros((P, C_COLS), f)
    consts[:, C_IDENT:C_IDENT + P] = np.eye(P, dtype=f)
    consts[:, C_IOTA:C_IOTA + WIN] = np.arange(WIN, dtype=f)
    for turn in range(TURNS):
        for k, at in enumerate(FLUSH_AT):
            consts[:, C_DUE + turn * BODY + at:] = max(0, (turn * 2 + k + 1 - LEAD) * P)
    fc1_w = np.zeros((BODY, BASIS, BODY, HID), f)
    for j in range(BODY):
        fc1_w[j, :, j] = L0_gnn_W_fc1

    def tiles(a, extra):
        t = a.reshape((TILES, P) + a.shape[1:])
        t = t.transpose((1, 0) + tuple(range(2, t.ndim)))
        return np.concatenate([t, t[:, :extra]], axis=1)

    src_p = padded(src, E)
    dst_p = np.concatenate([dst, np.repeat(dst[-1:], E - EDGES)])
    len_p = padded(lens, E).reshape(TURNS, BODY, QE, BASIS).transpose(1, 3, 0, 2).reshape(
        BODY * BASIS, TURNS * QE)

    arrays = {
        "x": by_direction(padded(x, NP)),
        "attr": np.concatenate([np.zeros((LEAD, P), f), padded(np.asarray(node_vec1), NP).reshape(CHUNKS, P)]).T,
        "node_w": node_w,
        "consts": consts,
        "fc1_w": fc1_w.reshape(BODY * BASIS, BODY, HID),
        "fc2_w": np.asarray(L0_gnn_W_fc2),
        "src_idx": tiles(src_p, AHEAD * TQ),
        "dst_tiles": tiles(dst_p, TQ),
        "dst_quads": dst_p.reshape(QUADS, QE),
        "edge_at": tiles(padded(ea, E), TQ),
        "lengths": np.concatenate([len_p, len_p[:, :QE]], axis=1),
    }
    arrays = {f"{k}_dram": np.ascontiguousarray(a) for k, a in arrays.items()}
    nc = bacc.Bacc("TRN2", target_bir_lowering=False, num_devices=1)
    args = [nc.dram_tensor(k, a.shape, mybir.dt.from_np(a.dtype), kind="ExternalInput").ap()
            for k, a in arrays.items()]
    y_table = nc.dram_tensor("y_table", (NP, FEAT), mybir.dt.float32, kind="Internal").ap()
    out = nc.dram_tensor("out_dram", (SLOTS_C * P, FEAT), mybir.dt.float32, kind="ExternalOutput").ap()
    edge_conv_program(nc, *args, y_table, out)
    o = run_bass_kernel_spmd(nc, [arrays], core_ids=[0]).results[0]["out_dram"][LEAD * P:LEAD * P + NODES]
    v = o[:, MUL:].reshape(NODES, 3, MUL).transpose(0, 2, 1).reshape(NODES, 3 * MUL)
    return np.concatenate([o[:, :MUL], v], axis=1)
```

```python
import math
from contextlib import ExitStack

import concourse.bass as bass
from concourse import mybir

P = 128
NODES, FEAT, MUL = 3125, 128, 32
EDGES, BASIS, HID = 53125, 10, 100
CHUNKS = -(-NODES // P)
NP = CHUNKS * P
TQ = 4
QE = TQ * P
QUADS = -(-EDGES // QE)
BODY = 8
SLOTS = 8
EARLY = 4
TURNS = QUADS // BODY
TILES = QUADS * TQ
LEAD = 3
SLOTS_C = CHUNKS + LEAD
FLUSH_AT = (1, 4)
PAIRS = SLOTS_C // 2
FIRST_PAIR = LEAD // 2
WIN = 42
NK = 4
AHEAD = 7
AGG_CUTS = (0, 24, 50, 76, 94)
LN_EPS = 1e-5
LEN_CUTS = (0, 2, 6, 10)
STD_AT = 3
WARM = 12
WARM_END = 1
ROUND_UP = 0.51

assert QUADS % BODY == 0 and SLOTS == BODY and EARLY < AHEAD < SLOTS
assert SLOTS_C == 2 * PAIRS and PAIRS > TURNS

C_SELF = math.sin(math.pi / 8) / math.sqrt(MUL)
C_AGG = (math.cos(math.pi / 8) / math.sqrt(2 * MUL) / math.sqrt(16.0)
         / math.sqrt(HID) / math.sqrt(MUL))
C_DOT = C_AGG / math.sqrt(3.0)
C_FC1 = 1.0 / math.sqrt(BASIS)

BATCHES = [(0, 4), (4, 8), (12, 13)]
GROUPS = [(c, min(4, CHUNKS - c)) for c in range(0, CHUNKS, 4)]

COLS = CHUNKS + EARLY * TQ
COL_BATCHES = BATCHES + [(CHUNKS + q * TQ, TQ) for q in range(EARLY)]
COL_GROUPS = GROUPS + [(CHUNKS + q * TQ, TQ) for q in range(EARLY)]
assert (len(GROUPS) - 2) % 3 == 2
BATCH_OF = [next(i for i, (b, m) in enumerate(COL_BATCHES) if b <= c < b + m) for c, _ in COL_GROUPS]

W_IN, W_SELF, W_AGG, W_DOT = 0, 128, 256, 384
W_COLS = W_DOT + 3 * 64
C_IDENT, C_NODE_W = 0, 128
C_FIRST = C_NODE_W + W_SELF
C_IOTA = C_NODE_W + W_COLS
C_DUE = C_IOTA + WIN
C_ATTR = C_DUE + QUADS
C_FC2 = C_ATTR + SLOTS_C
C_COLS = C_FC2 + P


def edge_conv_program(nc, x, consts, fc1_w, src_idx, dst_tiles, dst_quads,
                      edge_at, lengths, y_table, out):
    f32, i32 = mybir.dt.float32, mybir.dt.int32
    ALU = mybir.AluOpType
    ACT = mybir.ActivationFunctionType
    AX = mybir.AxisListType

    ctx = ExitStack()
    with ctx:
        def sb(name, shape, dt=f32):
            return ctx.enter_context(nc.sbuf_tensor(name, shape, dt))

        def pb(name):
            return ctx.enter_context(nc.psum_tensor(name, [P, 512], f32))

        def sem(name):
            return ctx.enter_context(nc.semaphore(name))

        out_sb = sb("out_sb", [P, SLOTS_C, FEAT])
        x_sb = out_sb[:, LEAD:, :]
        c_sb = sb("c_sb", [P, C_COLS])
        w_sb = c_sb[:, C_NODE_W:C_NODE_W + W_COLS]
        attr_all = c_sb[:, C_ATTR:C_ATTR + SLOTS_C]
        attr_sb = attr_all[:, LEAD:]
        fc2_sb = c_sb[0:HID, C_FC2:C_FC2 + P]
        stats = sb("stats", [P, COLS, 6])
        m_neg = sb("m_neg", [P, COLS])
        m_diff = sb("m_diff", [P, COLS])
        v_sum = sb("v_sum", [P, COLS])
        m_sq = sb("m_sq", [P, COLS])
        var = sb("var", [P, COLS])
        std = sb("std", [P, COLS])
        rstd = sb("rstd", [P, COLS])
        y_scale = sb("y_scale", [P, COLS])
        xn = sb("xn", [P, CHUNKS, FEAT])
        h_t = sb("h_t", [P, CHUNKS, P])
        y_sb = xn
        ones = sb("ones", [P, P])
        fc1_sb = sb("fc1_sb", [BODY * BASIS, BODY, HID])
        len_sb = sb("len_sb", [BODY * BASIS, (TURNS + 1) * QE])
        idx_sb = sb("idx_sb", [P, TILES + AHEAD * TQ], i32)
        idx_now = sb("idx_now", [P, SLOTS, TQ], i32)
        dst_sb = sb("dst_sb", [P, TILES + TQ], i32)
        dst_rel = sb("dst_rel", [P, TILES + TQ])
        ea_sb = sb("ea_sb", [P, TILES + TQ, NK])
        dq_sb = sb("dq_sb", [QUADS, QE], i32)
        q_min = sb("q_min", [QUADS, 1])
        q_max = sb("q_max", [QUADS, 1])
        q_span = sb("q_span", [QUADS, 1])
        diag = sb("diag", [QUADS, 2, QUADS])
        base_row = sb("base_row", [1, 1 + QUADS], i32)
        span_top = sb("span_top", [P, 1])
        rounds_sb = sb("rounds_sb", [P, 1], i32)
        slack = sb("slack", [P, QUADS])
        slack_min = sb("slack_min", [P, 1])
        one_round = sb("one_round", [P, 1])
        complete = sb("complete", [P, 1])
        again = sb("again", [P, 1], i32)
        h_sb = sb("h_sb", [HID, 2, QE])
        y_src = sb("y_src", [P, SLOTS, TQ, FEAT + 1])
        prod = sb("prod", [P, 2, TQ, 2, FEAT])
        sel = sb("sel", [P, 2, TQ, NK, WIN])
        agg = sb("agg", [P, NK, SLOTS_C * P])
        blank = sb("blank", [P, 1, 1])
        stage_sb = sb("stage_sb", [P, NK, 2, P])

        fc1_ps = [pb(f"fc1_ps{i}") for i in range(2)]
        w_ps = [pb(f"w_ps{i}") for i in range(2)]
        agg_ps = [pb(f"agg_ps{i}") for i in range(2)]
        win_ps = pb("win_ps")
        flush_ps = [pb("flush_ps"), win_ps]
        y_ps = w_ps + agg_ps
        self_ps = [flush_ps[0], win_ps, agg_ps[1]]

        s_x = [sem(f"s_x{i}") for i in range(len(BATCHES))]
        s_first = sem("s_first")
        s_const = sem("s_const")
        s_fc = sem("s_fc")
        s_idx = sem("s_idx")
        s_dst = sem("s_dst")
        s_dq = sem("s_dq")
        s_ea = sem("s_ea")
        s_len_first = sem("s_len_first")
        s_len = sem("s_len")
        s_ones = sem("s_ones")
        s_zero = sem("s_zero")
        s_chain = sem("s_chain")
        s_diag = sem("s_diag")
        s_win = sem("s_win")
        s_rounds = sem("s_rounds")
        s_mean = sem("s_mean")
        s_var = sem("s_var")
        s_std = sem("s_std")
        s_warm = sem("s_warm")
        s_xn = sem("s_xn")
        s_xt = sem("s_xt")
        s_ht = sem("s_ht")
        s_y = sem("s_y")
        s_ysb = sem("s_ysb")
        s_scaled = sem("s_scaled")
        s_early = sem("s_early")
        s_table = sem("s_table")
        s_self = sem("s_self")
        s_skip = sem("s_skip")
        s_wscaled = sem("s_wscaled")
        idx_staged = sem("idx_staged")
        y_free = sem("y_free")
        quads_begun = sem("quads_begun")
        gathered = [sem(f"gathered{j}") for j in range(SLOTS)]
        fc1_done = sem("fc1_done")
        silu_done = sem("silu_done")
        fc2_done = sem("fc2_done")
        sel_done = sem("sel_done")
        prod_a_done = sem("prod_a_done")
        prod_b_done = sem("prod_b_done")
        agg_done = sem("agg_done")
        summed = sem("summed")
        moved = sem("moved")
        s_blank = sem("s_blank")
        s_again = sem("s_again")
        staged = sem("staged")
        waits_met = sem("waits_met")
        cleared = sem("cleared")
        mapped = sem("mapped")
        flushed = sem("flushed")
        s_out = sem("s_out")
        landed = sem("landed")

        ident = c_sb[:, C_IDENT:C_IDENT + P]
        iota = c_sb[:, C_IOTA:C_IOTA + WIN]
        x_rows = x[:, 0:FEAT].rearrange("(c p) f -> p c f", p=P)
        y_early = y_src[:, 0:EARLY, :, :].rearrange("p q t f -> p (q t) f")

        def columns(chunks, c, n):
            if c < CHUNKS:
                return chunks[:, c:c + n, :]
            return y_early[:, c - CHUNKS:c - CHUNKS + n, 0:FEAT]

        y_rows = y_table.rearrange("(c p) f -> p c f", p=P)
        out_rows = out.rearrange("(c p) f -> p c f", p=P)

        def last_pairs(pair):
            return nc.s_assert_within(
                pair, FIRST_PAIR, PAIRS - 1,
                skip_runtime_bounds_check_because="the loop over them ends at PAIRS")

        def clear_agg(engine, part):
            cuts = [c * P // 4 for c in AGG_CUTS] + [SLOTS_C * P]
            where = agg[:, :, cuts[part]:cuts[part + 1]]
            if engine is not nc.scalar:
                engine.memset(where, 0.0).then_inc(s_zero, 1)
            else:
                engine.memzero(where).then_inc(s_zero, 1)

        block = ctx.enter_context(nc.Block())

        @block.sync
        def _(sp):
            def load_x(i):
                c, n = BATCHES[i]
                sp.dma_start(x_sb[:, c:c + n, :], x_rows[:, c:c + n, :]).then_inc(s_x[i], 16)

            def load_lengths(i):
                cols = slice(LEN_CUTS[i] * QE, (LEN_CUTS + (TURNS + 1,))[i + 1] * QE)
                sp.dma_start(len_sb[:, cols], lengths[:, cols]).then_inc(s_len if i else s_len_first, 16)

            sp.sem_inc(s_out, 16)
            sp.dma_start(idx_sb[:, :], src_idx).then_inc(s_idx, 16)
            load_x(0)
            sp.dma_start(c_sb[:, 0:C_FIRST], consts[:, 0:C_FIRST]).then_inc(s_first, 16)
            load_x(1)
            load_x(2)
            sp.dma_start(c_sb[:, C_FIRST:], consts[:, C_FIRST:]).then_inc(s_const, 16)
            sp.dma_start(dq_sb[:, :], dst_quads).then_inc(s_dq, 16)
            sp.dma_start(dst_sb[:, :], dst_tiles).then_inc(s_dst, 16)
            sp.dma_start(fc1_sb[:, :, :], fc1_w).then_inc(s_fc, 16)
            load_lengths(0)
            for g, (c, n) in enumerate(GROUPS):
                sp.wait_ge(s_ysb, g + 1)
                sp.dma_start(y_rows[:, c:c + n, :], y_sb[:, c:c + n, :]).then_inc(s_table, 16)
            sp.dma_start(ea_sb[:, :, :], edge_at).then_inc(s_ea, 16)
            for i in range(1, len(LEN_CUTS)):
                load_lengths(i)
            sp.wait_ge(s_again, 1)
            rounds = nc.sync.value_load(rounds_sb[0:1, 0:1], min_val=1, max_val=NP)
            first = nc.sync.value_load(again[0:1, 0:1], min_val=FIRST_PAIR, max_val=TURNS)
            with nc.sync.Fori(0, rounds) as r:
                with nc.sync.Fori(0, TURNS) as b:
                    turn = r * TURNS + b
                    sp.wait_ge(flushed, turn * 2 + 4)
                    sp.wait_ge(s_out, turn * 16 + 16)
                    sp.dma_start(out_rows[:, bass.ds(b * 2, 2), :],
                                 out_sb[:, bass.ds(b * 2, 2), :]).then_inc(s_out, 16)
            stores = rounds * TURNS + 1
            sp.wait_ge(s_out, stores * 16)
            sp.sem_inc(landed, 1)
            with nc.sync.Fori(0, PAIRS - first) as k:
                sp.wait_ge(flushed, (rounds * TURNS + k) * 2 + 4)
                c = last_pairs(first + k) * 2
                sp.dma_start(out_rows[:, bass.ds(c, 2), :],
                             out_sb[:, bass.ds(c, 2), :]).then_inc(s_out, 16)
                sp.wait_ge(s_out, stores * 16 + k * 16 + 16)
                sp.sem_inc(landed, 1)

        @block.gpsimd
        def _(pool):
            nc.gpsimd.memset(blank[:, :, :], 0.0).then_inc(s_blank, 1)
            clear_agg(nc.gpsimd, 0)
            pool.wait_ge(s_idx, 16)
            for q in range(EARLY):
                for t in range(TQ):
                    pool.indirect_dma_start(
                        y_src[:, q, t, :], None, x[:, :],
                        bass.IndirectOffsetOnAxis(idx_sb[:, q * TQ + t:q * TQ + t + 1], 0),
                    ).then_inc(gathered[q], 16)
            nc.gpsimd.memset(out_sb[:, 0:LEAD, :], 0.0).then_inc(s_blank, 1)
            clear_agg(nc.gpsimd, 3)

            def gather(j, step):
                pool.wait_ge(idx_staged, step + 1)
                pool.wait_ge(y_free, step + 1)
                pool.sem_inc(quads_begun, 1)
                slot = (j + EARLY) % SLOTS
                for t in range(TQ):
                    pool.indirect_dma_start(
                        y_src[:, slot, t, 0:FEAT], None, y_table[:, :],
                        bass.IndirectOffsetOnAxis(idx_now[:, slot, t:t + 1], 0),
                    ).then_inc(gathered[slot], 16)

            pool.wait_ge(s_rounds, 1)
            rounds = nc.gpsimd.value_load(rounds_sb[0:1, 0:1], min_val=1, max_val=NP)
            pool.wait_ge(s_table, 16 * len(GROUPS))
            with nc.gpsimd.Fori(1, rounds * TURNS) as b:
                for j in range(BODY):
                    gather(j, b * BODY + j)
            for j in range(BODY - EARLY):
                gather(j, rounds * QUADS + j)

        @block.scalar
        def _(act):
            nc.scalar.preload_act_table(ACT.Sqrt)
            clear_agg(nc.scalar, 2)

            def stage(q_col, slot):
                nc.scalar.copy(idx_now[:, slot, :], idx_sb[:, q_col]).then_inc(idx_staged, 1)

            act.wait_ge(s_idx, 16)
            act.sem_inc(idx_staged, BODY)
            for q in range(EARLY, AHEAD):
                stage(slice(q * TQ, (q + 1) * TQ), q)

            def centre(g):
                c, n = COL_GROUPS[g]
                act.wait_ge(s_mean, BATCH_OF[g] + 1)
                for k in range(c, c + n):
                    nc.scalar.activation(columns(xn, k, 1), columns(x_sb, k, 1), ACT.Identity,
                                         bias=m_neg[:, k:k + 1], scale=2.0).then_inc(s_xn, 1)

            def relu(g):
                c, n = COL_GROUPS[g]
                act.wait_ge(s_xt, g + 1)
                nc.scalar.activation(columns(h_t, c, n),
                                     fc1_ps[g % 2][:, 0:n * P].rearrange("p (n f) -> p n f", f=P),
                                     ACT.Relu).then_inc(s_ht, 1)

            def deviations(c, n, count):
                act.wait_ge(s_var, count)
                nc.scalar.activation(std[:, c:c + n], var[:, c:c + n], ACT.Sqrt).then_inc(s_std, 1)

            for g in range(len(GROUPS)):
                centre(g)
                if g == STD_AT:
                    deviations(0, CHUNKS, 1)
                if g >= 1:
                    relu(g - 1)
            relu(len(GROUPS) - 1)
            for g in range(len(GROUPS), len(COL_GROUPS)):
                centre(g)
                if g == len(COL_GROUPS) - 1:
                    deviations(CHUNKS, EARLY * TQ, 2)
                relu(g)

            def early_rows(q):
                c, n = COL_GROUPS[len(GROUPS) + q]
                act.wait_ge(s_y, len(GROUPS) + q + 1)
                for k in range(n):
                    last = nc.scalar.activation(y_early[:, c + k - CHUNKS, 0:FEAT],
                                                y_ps[(len(GROUPS) + q) % 4][:, k * P:(k + 1) * P],
                                                ACT.Copy, scale=y_scale[:, c + k:c + k + 1])
                last.then_inc(s_early, 1)

            def silu(i):
                nc.scalar.activation(h_sb[:, i, :], fc1_ps[i][0:HID, :], ACT.Silu,
                                     scale=C_FC1).then_inc(silu_done, 1)

            act.wait_ge(s_scaled, 1)
            for q in range(EARLY):
                early_rows(q)
                if q == 1:
                    nc.scalar.preload_act_table(ACT.Silu)
                    act.wait_ge(fc1_done, 1)
                    silu(0)
            clear_agg(nc.scalar, 4)
            act.wait_ge(s_rounds, 1)
            rounds = nc.scalar.value_load(rounds_sb[0:1, 0:1], min_val=1, max_val=NP)
            with nc.scalar.Fori(0, rounds) as r:
                with nc.scalar.Fori(0, TURNS) as b:
                    for j in range(BODY):
                        step = r * QUADS + b * BODY + j
                        act.wait_ge(fc1_done, step + 2)
                        silu((j + 1) % 2)
                        act.wait_ge(y_free, step + BODY + AHEAD + 1 - EARLY)
                        stage(bass.ds((b * BODY + j + AHEAD) * TQ, TQ), (j + AHEAD) % SLOTS)

        @block.vector
        def _(dve):
            links = [0]

            def link(ins):
                links[0] += 1
                ins.then_inc(s_chain, 1)
                dve.wait_ge(s_chain, links[0])

            def statistics(i):
                c, n = COL_BATCHES[i]
                if c < CHUNKS:
                    dve.wait_ge(s_x[i], 16)
                else:
                    dve.wait_ge(gathered[(c - CHUNKS) // TQ], 16 * TQ)
                for k in range(c, c + n):
                    last = nc.vector.bn_stats(stats[:, k, :], columns(x_sb, k, 1).rearrange("p o f -> p (o f)"))
                link(last)
                nc.vector.scalar_tensor_tensor(m_neg[:, c:c + n], stats[:, c:c + n, 1], -1.0,
                                               stats[:, c:c + n, 4], ALU.mult,
                                               ALU.subtract).then_inc(s_mean, 1)

            def variances(c, n):
                cs = slice(c, c + n)
                m0, v0, m1, v1 = (stats[:, cs, k] for k in (1, 2, 4, 5))
                nc.vector.tensor_tensor(v_sum[:, cs], v0, v1, ALU.add)
                link(nc.vector.tensor_tensor(m_diff[:, cs], m0, m1, ALU.subtract))
                nc.vector.tensor_scalar(v_sum[:, cs], v_sum[:, cs], 1.0 / FEAT, LN_EPS, ALU.mult, ALU.add)
                link(nc.vector.scalar_tensor_tensor(m_sq[:, cs], m_diff[:, cs], 0.25, m_diff[:, cs],
                                                    ALU.mult, ALU.mult))
                nc.vector.tensor_tensor(var[:, cs], m_sq[:, cs], v_sum[:, cs], ALU.add).then_inc(s_var, 1)

            def scales(c, n, attr_of, count):
                cs = slice(c, c + n)
                dve.wait_ge(s_std, count)
                link(nc.vector.reciprocal(rstd[:, cs], std[:, cs]))
                link(nc.vector.scalar_tensor_tensor(y_scale[:, cs], rstd[:, cs], 0.5, attr_of,
                                                    ALU.mult, ALU.mult))

            def table(g):
                c, n = COL_GROUPS[g]
                dve.wait_ge(s_y, g + 1)
                nc.vector.tensor_tensor(
                    columns(y_sb, c, n), y_ps[g % 4][:, 0:n * P].rearrange("p (c f) -> p c f", f=FEAT),
                    y_scale[:, c:c + n].unsqueeze(2).to_broadcast([P, n, FEAT]), ALU.mult).then_inc(s_ysb, 1)

            nc.vector.memset(ones[:, :], 1.0).then_inc(s_ones, 1)
            clear_agg(nc.vector, 1)
            dve.sem_inc(y_free, BODY + SLOTS - EARLY)
            dve.sem_inc(summed, 1)
            nb, ng = len(BATCHES), len(GROUPS)
            for i in range(nb):
                statistics(i)
            variances(0, CHUNKS)
            dve.wait_ge(s_const, 16)
            nc.vector.tensor_scalar(w_sb[:, W_SELF:W_AGG], w_sb[:, W_SELF:W_AGG], C_SELF, None,
                                    ALU.mult).then_inc(s_wscaled, 1)
            dve.wait_ge(s_dq, 16)
            nc.vector.tensor_reduce(q_min[:, :], dq_sb[:, :], AX.X, ALU.min)
            link(nc.vector.tensor_reduce(q_max[:, :], dq_sb[:, :], AX.X, ALU.max))
            link(nc.vector.tensor_tensor(q_span[:, :], q_max[:, :], q_min[:, :], ALU.subtract))
            for a, ends in enumerate((q_min, q_span)):
                last = nc.vector.tensor_scalar(diag[:, a, :], ident[0:QUADS, 0:QUADS], ends[:, 0:1], None,
                                               ALU.mult)
            last.then_inc(s_diag, 1)
            scales(0, CHUNKS, attr_sb, 1)
            for g in range(3):
                table(g)
            statistics(nb)
            for g in range(3, ng):
                table(g)
            statistics(nb + 1)

            dve.wait_ge(s_win, 1)
            nc.vector.tensor_scalar(base_row[:, 1:], win_ps[0:1, 0:QUADS], float(LEAD * P - WIN), None,
                                    ALU.add)
            nc.vector.tensor_tensor(slack[:, :], win_ps[:, 0:QUADS], c_sb[:, C_DUE:C_DUE + QUADS],
                                    ALU.subtract)
            link(nc.vector.tensor_reduce(span_top[:, :], win_ps[:, QUADS:2 * QUADS], AX.X, ALU.max))
            nc.vector.tensor_scalar(rounds_sb[:, :], span_top[:, :], 1.0 / WIN, ROUND_UP,
                                    ALU.mult, ALU.add).then_inc(s_rounds, 1)
            nc.vector.tensor_scalar(one_round[:, :], span_top[:, :], float(WIN), float(TURNS - FIRST_PAIR),
                                    ALU.is_lt, ALU.mult)
            link(nc.vector.tensor_reduce(slack_min[:, :], slack[:, :], AX.X, ALU.min))
            link(nc.vector.scalar_tensor_tensor(complete[:, :], slack_min[:, :], 0.0, one_round[:, :],
                                                ALU.is_ge, ALU.mult))
            nc.vector.tensor_scalar(again[:, :], complete[:, :], float(FIRST_PAIR), None,
                                    ALU.add).then_inc(s_again, 1)

            for q in range(2, EARLY):
                statistics(nb + q)
            variances(CHUNKS, EARLY * TQ)

            dve.wait_ge(s_dst, 16)
            nc.vector.tensor_tensor(
                dst_rel[:, 0:TILES].rearrange("p (q t) -> p q t", t=TQ),
                dst_sb[:, 0:TILES].rearrange("p (q t) -> p q t", t=TQ),
                win_ps[:, 0:QUADS].unsqueeze(2).to_broadcast([P, QUADS, TQ]), ALU.subtract)
            link(nc.vector.tensor_tensor(dst_rel[:, TILES:], dst_sb[:, TILES:],
                                         win_ps[:, 0:1].to_broadcast([P, TQ]), ALU.subtract))
            link(nc.vector.tensor_scalar(dst_rel[:, 0:TILES], dst_rel[:, 0:TILES], float(WIN), None,
                                         ALU.add))
            nc.vector.tensor_scalar(w_sb[:, W_AGG:W_DOT], w_sb[:, W_AGG:W_DOT], C_AGG, None, ALU.mult)
            for lo, hi, scale in ((0, 32, C_AGG), (32, 64, C_DOT), (64, 128, C_DOT)):
                last = nc.vector.tensor_scalar(w_sb[lo:hi, W_DOT:], w_sb[lo:hi, W_DOT:], scale, None,
                                               ALU.mult)
            last.then_inc(s_wscaled, 1)

            def build_sel(col, i):
                for t in range(TQ):
                    last = nc.vector.scalar_tensor_tensor(
                        sel[:, i, t, :, :],
                        iota.unsqueeze(1).to_broadcast([P, NK, WIN]),
                        dst_rel[:, bass.ds(col + t, 1)],
                        ea_sb[:, bass.ds(col + t, 1), :].rearrange("p o k -> p (o k)").unsqueeze(2)
                        .to_broadcast([P, NK, WIN]),
                        ALU.is_equal, ALU.mult)
                last.then_inc(sel_done, 1)

            scales(CHUNKS, EARLY * TQ, y_early[:, :, FEAT], 2)
            dve.sem_inc(s_scaled, 1)

            dve.wait_ge(s_ea, 16)
            build_sel(TILES, 0)

            dve.wait_ge(s_rounds, 1)
            dve.wait_ge(s_again, 1)
            rounds = nc.vector.value_load(rounds_sb[0:1, 0:1], min_val=1, max_val=NP)

            for g, (c, n) in enumerate(GROUPS):
                dve.wait_ge(s_self, g + 1)
                ps = self_ps[g % 3]
                for k in range(n):
                    last = nc.vector.scalar_tensor_tensor(
                        x_sb[:, c + k, :], ps[:, k * P:(k + 1) * P], y_scale[:, c + k:c + k + 1],
                        x_sb[:, c + k, :], ALU.mult, ALU.add)
                last.then_inc(s_skip, 1)
                if g == len(GROUPS) - 2:
                    dve.wait_ge(s_skip, g + 1)
                    nc.vector.memset(agg_ps[1][:, 0:NK * WIN], 0.0).then_inc(agg_done, 1)

            dve.wait_ge(s_zero, 5)
            dve.wait_ge(s_early, EARLY)

            def add_sums(base, i, step):
                dve.wait_ge(agg_done, step + 1)
                dve.wait_ge(summed, step + 1)
                here = agg[:, :, bass.ds(base, WIN)]
                nc.vector.tensor_tensor(
                    here, here, agg_ps[i][:, 0:NK * WIN].rearrange("p (k n) -> p k n", k=NK),
                    ALU.add).then_inc(summed, 1)

            def stage(c, half, n, adds):
                dve.wait_ge(mapped, n)
                dve.wait_ge(summed, adds)
                dve.sem_inc(waits_met, 1)
                nc.vector.tensor_copy(stage_sb[:, :, half, :],
                                      agg[:, :, bass.ds(c * P, P)]).then_inc(staged, 1)

            def clear(c, n):
                dve.wait_ge(staged, n)
                dve.sem_inc(waits_met, 1)
                nc.vector.tensor_copy(agg[:, :, bass.ds(c * P, P)],
                                      blank[:, :, :].to_broadcast([P, NK, P])).then_inc(cleared, 1)
                dve.wait_ge(cleared, n)

            def to_output(c, half, n, turn):
                dve.wait_ge(mapped, n + 2)
                dve.wait_ge(flushed, n + 1)
                dve.wait_ge(s_out, turn * 16 + 16)
                rows = out_sb[:, bass.ds(c, 1), :].rearrange("p o f -> p (o f)")
                nc.vector.scalar_tensor_tensor(
                    rows, flush_ps[half][:, 0:P], attr_all[:, bass.ds(c, 1)], rows,
                    ALU.mult, ALU.add).then_inc(flushed, 1)

            dve.sem_inc(mapped, 2)
            dve.sem_inc(flushed, 2)
            dve.wait_ge(s_blank, 2)
            with nc.vector.Fori(0, rounds) as r:
                dve.wait_ge(sel_done, r * QUADS + 1)
                nc.vector.tensor_scalar(dst_rel[:, :], dst_rel[:, :], float(WIN), None,
                                        ALU.subtract).then_inc(moved, 1)
                nc.vector.tensor_copy(base_row[:, 0:1], base_row[:, QUADS:]).then_inc(moved, 1)
                dve.wait_ge(moved, r * 3 + 2)
                nc.vector.tensor_scalar(base_row[:, 1:], base_row[:, 1:], float(WIN), float(SLOTS_C * P - WIN),
                                        ALU.add, ALU.min).then_inc(moved, 1)
                dve.wait_ge(moved, r * 3 + 3)
                dve.sem_inc(waits_met, 1)
                with nc.vector.Fori(0, TURNS) as b:
                    turn = r * TURNS + b
                    for j in range(BODY):
                        i = j % 2
                        quad = b * BODY + j
                        step = r * QUADS + quad
                        base = nc.vector.value_load(base_row[0:1, bass.ds(quad, 1)],
                                                    min_val=0, max_val=SLOTS_C * P - WIN)
                        if j == BODY - 1:
                            last_base = nc.vector.value_load(base_row[0:1, QUADS:QUADS + 1],
                                                             min_val=0, max_val=SLOTS_C * P - WIN)
                            first = nc.vector.value_load(again[0:1, 0:1], min_val=FIRST_PAIR, max_val=TURNS)
                        dve.wait_ge(fc2_done, step + 1)
                        dve.wait_ge(gathered[j], turn * (16 * TQ) + 16 * TQ)
                        w = w_ps[i][:, :].rearrange("p (t k u) -> p t k u", t=TQ, k=4)
                        y = y_src[:, j, :, 0:FEAT].rearrange("p t (k u) -> p t k u", k=4)
                        pr = prod[:, i, :, :, :].rearrange("p t a (k u) -> p t a k u", k=4)
                        nc.vector.tensor_tensor(
                            pr[:, :, :, 0, :], w[:, :, 0:2, :],
                            y[:, :, 0:1, :].to_broadcast([P, TQ, 2, MUL]), ALU.mult)
                        nc.vector.tensor_tensor(
                            pr[:, :, 0, 1:4, :], w[:, :, 2:3, :].to_broadcast([P, TQ, 3, MUL]),
                            y[:, :, 1:4, :], ALU.mult).then_inc(prod_a_done, 1)
                        nc.vector.tensor_tensor(
                            pr[:, :, 1, 1:4, :], w[:, :, 3:4, :].to_broadcast([P, TQ, 3, MUL]),
                            y[:, :, 1:4, :], ALU.mult).then_inc(prod_b_done, 1)
                        add_sums(base, 1 - i, step)
                        dve.wait_ge(prod_b_done, step + 1)
                        dve.sem_inc(y_free, 1)
                        build_sel((quad + 1) * TQ, (j + 1) % 2)
                        for k, at in enumerate(FLUSH_AT):
                            n = turn * 2 + k + 1
                            if j == at:
                                stage(b * 2 + k, k, n, step + 2)
                                clear(b * 2 + k, n)
                            if j == at + 2:
                                to_output(b * 2 + k, k, n, turn)
            add_sums(last_base, (QUADS - 1) % 2, rounds * QUADS)

            with nc.vector.Fori(0, PAIRS - first) as k:
                n = (rounds * TURNS + k) * 2 + 1
                c = last_pairs(first + k) * 2
                for half in range(2):
                    stage(c + half, half, n + half, rounds * QUADS + 2)
                for half in range(2):
                    to_output(c + half, half, n + half, rounds * TURNS)

        @block.tensor
        def _(pe):
            pe.wait_ge(s_ones, 1)
            for _ in range(WARM):
                last = nc.tensor.matmul(win_ps[:, 0:P], ones[:, :], ones[:, :], start=True, stop=True)
            last.then_inc(s_warm, 1)
            pe.wait_ge(s_first, 16)
            ng = len(COL_GROUPS)

            def transposes(g):
                c, n = COL_GROUPS[g]
                if g >= 2:
                    pe.wait_ge(s_ht, g - 1)
                for k in range(n):
                    pe.wait_ge(s_xn, c + k + 1)
                    last = nc.tensor.transpose(fc1_ps[g % 2][:, k * P:(k + 1) * P],
                                               columns(xn, c + k, 1).rearrange("p o f -> p (o f)"), ident)
                last.then_inc(s_xt, 1)

            def maps(g):
                c, n = COL_GROUPS[g]
                pe.wait_ge(s_ht, g + 1)
                if g >= 4:
                    pe.wait_ge(s_ysb, g - 3)
                for k in range(n):
                    last = nc.tensor.matmul(y_ps[g % 4][:, k * P:(k + 1) * P],
                                            columns(h_t, c + k, 1).rearrange("p o f -> p (o f)"),
                                            w_sb[:, W_IN:W_IN + P], start=True, stop=True)
                last.then_inc(s_y, 1)

            for g in range(len(GROUPS)):
                transposes(g)
                if g:
                    maps(g - 1)
            maps(len(GROUPS) - 1)

            pe.wait_ge(s_diag, 1)
            pe.wait_ge(s_warm, 1)
            nc.tensor.matmul(win_ps[:, 0:2 * QUADS], ones[0:QUADS, :],
                             diag[:, :, :].rearrange("q a n -> q (a n)"),
                             start=True, stop=True).then_inc(s_win, 1)

            def self_maps(g):
                c, n = GROUPS[g]
                if g == 1:
                    pe.wait_ge(s_wscaled, 2)
                if g == 2:
                    pe.wait_ge(s_early, 1)
                if g >= 3:
                    pe.wait_ge(s_skip, g - 2)
                for k in range(n):
                    last = nc.tensor.matmul(self_ps[g % 3][:, k * P:(k + 1) * P], h_t[:, c + k, :],
                                            w_sb[:, W_SELF:W_SELF + P], start=True, stop=True)
                last.then_inc(s_self, 1)

            pe.wait_ge(s_wscaled, 1)
            for g in range(len(GROUPS), ng):
                transposes(g)
                if g >= ng - 2:
                    self_maps(g - (ng - 2))
                maps(g)

            def fc1(col, group, i):
                nc.tensor.matmul(fc1_ps[i][0:HID, :], fc1_sb[:, group, :], len_sb[:, col],
                                 start=True, stop=True).then_inc(fc1_done, 1)

            def fc2(i):
                for t in range(TQ):
                    last = nc.tensor.matmul(w_ps[i][:, t * P:(t + 1) * P], h_sb[:, i, t * P:(t + 1) * P],
                                            fc2_sb[:, :], start=True, stop=True)
                last.then_inc(fc2_done, 1)

            pe.wait_ge(s_rounds, 1)
            pe.wait_ge(s_again, 1)
            rounds = nc.tensor.value_load(rounds_sb[0:1, 0:1], min_val=1, max_val=NP)
            first = nc.tensor.value_load(again[0:1, 0:1], min_val=FIRST_PAIR, max_val=TURNS)
            pe.wait_ge(s_fc, 16)
            pe.wait_ge(s_len_first, 16)
            pe.wait_ge(s_ht, ng)
            fc1(slice(0, QE), 0, 0)
            for g in range(2, 5):
                self_maps(g)
            fc1(slice(0, QE), 1, 1)
            pe.wait_ge(s_early, 2)
            pe.wait_ge(silu_done, 1)
            fc2(0)
            for g in range(5, len(GROUPS)):
                self_maps(g)
            pe.wait_ge(s_skip, len(GROUPS))
            pe.wait_ge(s_early, EARLY)

            def linear(half, n):
                pe.wait_ge(staged, n)
                pe.wait_ge(flushed, n)
                o = flush_ps[half][:, 0:P]
                nc.tensor.matmul(o, stage_sb[:, 0, half, :], w_sb[:, W_AGG:W_AGG + P], start=True, stop=False)
                for d in range(3):
                    cols = o.rearrange("p (k u) -> p k u", k=4)[:, 0:d + 2:d + 1, :]
                    wd = w_sb[:, W_DOT + 64 * d:W_DOT + 64 * (d + 1)].rearrange("p (k u) -> p k u", k=2)
                    last = nc.tensor.matmul(cols, stage_sb[:, 1 + d, half, :], wd, start=False, stop=(d == 2))
                last.then_inc(mapped, 1)

            pe.wait_ge(s_len, 16 * (len(LEN_CUTS) - 1))
            with nc.tensor.Fori(0, rounds) as r:
                with nc.tensor.Fori(0, TURNS) as b:
                    for j in range(BODY):
                        i = j % 2
                        step = r * QUADS + b * BODY + j
                        pe.wait_ge(silu_done, step + 2)
                        fc2((j + 1) % 2)
                        fc1(bass.ds((b + (j + 2) // BODY) * QE, QE), (j + 2) % BODY, i)
                        pe.wait_ge(sel_done, step + 1)
                        pe.wait_ge(prod_a_done, step + 1)
                        for t in range(TQ):
                            nc.tensor.matmul(agg_ps[i][:, 0:WIN], prod[:, i, t, 0, :], sel[:, i, t, 0, :],
                                             start=(t == 0), stop=(t == TQ - 1))
                        pe.wait_ge(prod_b_done, step + 1)
                        for t in range(TQ):
                            last = nc.tensor.matmul(agg_ps[i][:, WIN:NK * WIN], prod[:, i, t, 1, :],
                                                    sel[:, i, t, 1:NK, :].rearrange("p k n -> p (k n)"),
                                                    start=(t == 0), stop=(t == TQ - 1))
                        last.then_inc(agg_done, 1)
                        for k, at in enumerate(FLUSH_AT):
                            if j == at + 1:
                                linear(k, (r * TURNS + b) * 2 + k + 1)
            for _ in range(WARM_END):
                last = nc.tensor.matmul(w_ps[1][:, :], ones[:, :], h_t[:, 0:4, :].rearrange("p c f -> p (c f)"),
                                        start=True, stop=True)
            last.then_inc(s_warm, 1)
            with nc.tensor.Fori(0, PAIRS - first) as k:
                for half in range(2):
                    linear(half, (rounds * TURNS + k) * 2 + half + 1)


def kernel(x, src, dst, edge_attr_10, edge_attr_4, node_vec1, L0_gnn_W_sc0, L0_gnn_W_sc1,
           L0_gnn_W_l10, L0_gnn_W_l11, L0_gnn_W_l20, L0_gnn_W_l21, L0_gnn_W_fc1, L0_gnn_W_fc2):
    import numpy as np
    import concourse.bacc as bacc
    from concourse.bass_utils import run_bass_kernel_spmd

    f = np.float32

    def by_direction(a):
        v = a[:, MUL:].reshape(-1, MUL, 3).transpose(0, 2, 1).reshape(-1, 3 * MUL)
        return np.concatenate([a[:, :MUL], v], axis=1)

    def padded(a, rows):
        o = np.zeros((rows,) + a.shape[1:], a.dtype)
        o[:a.shape[0]] = a
        return o

    def blocks(w0, w1):
        o = np.zeros((FEAT, FEAT), f)
        for k, w in enumerate((w0, w1, w1, w1)):
            o[k * MUL:(k + 1) * MUL, k * MUL:(k + 1) * MUL] = w
        return o

    x, src, dst = np.asarray(x), np.asarray(src), np.asarray(dst)
    ea, lens = np.asarray(edge_attr_4), np.asarray(edge_attr_10)
    w20, w21 = np.asarray(L0_gnn_W_l20), np.asarray(L0_gnn_W_l21)
    E = QUADS * QE

    consts = np.zeros((P, C_COLS), f)
    node_w = consts[:, C_NODE_W:C_NODE_W + W_COLS]
    node_w[:, W_IN:W_IN + P] = blocks(L0_gnn_W_l10, L0_gnn_W_l11)
    node_w[:, W_SELF:W_SELF + P] = blocks(L0_gnn_W_sc0, L0_gnn_W_sc1)
    node_w[:, W_AGG:W_AGG + P] = blocks(w20[:MUL], w21[MUL:])
    for d in range(3):
        c = W_DOT + 64 * d
        node_w[MUL * (d + 1):MUL * (d + 2), c:c + MUL] = w20[MUL:]
        node_w[:MUL, c + MUL:c + 2 * MUL] = w21[:MUL]
    consts[:, C_ATTR + LEAD:C_ATTR + SLOTS_C] = padded(np.asarray(node_vec1), NP).reshape(CHUNKS, P).T
    consts[:HID, C_FC2:C_FC2 + P] = L0_gnn_W_fc2
    consts[:, C_IDENT:C_IDENT + P] = np.eye(P, dtype=f)
    consts[:, C_IOTA:C_IOTA + WIN] = np.arange(WIN, dtype=f)
    for turn in range(TURNS):
        for k, at in enumerate(FLUSH_AT):
            consts[:, C_DUE + turn * BODY + at:C_DUE + QUADS] = max(0, (turn * 2 + k + 1 - LEAD) * P)
    fc1_w = np.zeros((BODY, BASIS, BODY, HID), f)
    for j in range(BODY):
        fc1_w[j, :, j] = L0_gnn_W_fc1

    def tiles(a, extra):
        t = a.reshape((TILES, P) + a.shape[1:])
        t = t.transpose((1, 0) + tuple(range(2, t.ndim)))
        return np.concatenate([t, t[:, :extra]], axis=1)

    src_p = padded(src, E)
    dst_p = np.concatenate([dst, np.repeat(dst[-1:], E - EDGES)])
    len_p = padded(lens, E).reshape(TURNS, BODY, QE, BASIS).transpose(1, 3, 0, 2).reshape(
        BODY * BASIS, TURNS * QE)

    arrays = {
        "x": np.concatenate([by_direction(padded(x, NP)), padded(np.asarray(node_vec1), NP)], axis=1),
        "consts": consts,
        "fc1_w": fc1_w.reshape(BODY * BASIS, BODY, HID),
        "src_idx": tiles(src_p, AHEAD * TQ),
        "dst_tiles": tiles(dst_p, TQ),
        "dst_quads": dst_p.reshape(QUADS, QE),
        "edge_at": tiles(padded(ea, E), TQ),
        "lengths": np.concatenate([len_p, len_p[:, :QE]], axis=1),
    }
    arrays = {f"{k}_dram": np.ascontiguousarray(a) for k, a in arrays.items()}
    nc = bacc.Bacc("TRN2", target_bir_lowering=False, num_devices=1)
    args = [nc.dram_tensor(k, a.shape, mybir.dt.from_np(a.dtype), kind="ExternalInput").ap()
            for k, a in arrays.items()]
    y_table = nc.dram_tensor("y_table", (NP, FEAT), mybir.dt.float32, kind="Internal").ap()
    out = nc.dram_tensor("out_dram", (SLOTS_C * P, FEAT), mybir.dt.float32, kind="ExternalOutput").ap()
    edge_conv_program(nc, *args, y_table, out)
    o = run_bass_kernel_spmd(nc, [arrays], core_ids=[0]).results[0]["out_dram"][LEAD * P:LEAD * P + NODES]
    v = o[:, MUL:].reshape(NODES, 3, MUL).transpose(0, 2, 1).reshape(NODES, 3 * MUL)
    return np.concatenate([o[:, :MUL], v], axis=1)
```
